# Optimizing a Trainium2 kernel written in Bass

```python
import numpy as np
import jax
import jax.numpy as jnp

def _softmax(x, axis=-1):
    return jax.nn.softmax(x, axis=axis)

def _gelu(x):
    return jax.nn.gelu(x, approximate=True)

def _silu(x):
    return jax.nn.silu(x)

def _sigmoid(x):
    return jax.nn.sigmoid(x)

def _layernorm(x, axis=-1, eps=1e-05):
    m = jnp.mean(x, axis=axis, keepdims=True)
    v = jnp.var(x, axis=axis, keepdims=True)
    return (x - m) / jnp.sqrt(v + eps)

def _scatter_add(tgt, idx, src, axis=0):
    return tgt.at[idx].add(src)

def _segment_sum(src, seg, n):
    return jax.ops.segment_sum(src, seg, n)
kernel_name = 'mk_vit_tower_d1_tok_img256_r4_03aa33'

def setup_inputs(seed: int=0):
    np.random.seed(seed)
    _w = jnp.asarray

    def _rec_inputs():
        import jax
        import jax.numpy as jnp
        _rk = jax.random.key(seed)
        x = -7.10856e-05 + 0.999911 * jax.random.normal(jax.random.fold_in(_rk, 1), (2, 64, 128, 64), jnp.float32)
        return x
    x = _rec_inputs()

    def _L0_tok_setup():
        import jax, jax.numpy as jnp
        import numpy as np
        PATCH_LEN = 16
        STRIDE = 8
        PAD = 8
        key = jax.random.key(seed)
        k1, k2 = jax.random.split(key)
        x = jax.random.normal(k1, (32, 64, 128, 64), dtype=jnp.float32)
        in_feat = 64 * (PATCH_LEN // 2 + 1) * 2
        W = jax.random.normal(k2, (64, in_feat), dtype=jnp.float32) * 0.02
        return {'x': x, 'W': W}
    _L0_tok_all = _L0_tok_setup()
    _L0_tok_in = {k: v for k, v in _L0_tok_all.items() if k in ('W',)}
    del _L0_tok_all

    def _L0_attn_setup():
        import jax, jax.numpy as jnp
        import numpy as np
        D_MODEL = 64
        D_INNER = 128
        N_STATE = 64
        DT_RANK = 16
        K = 4
        B, L = (2, 256)

        def _selective_scan(u, delta, A, Bm, Cm, Dv):
            dA = jnp.einsum('bld,dn->bldn', delta, A)
            dB_u = jnp.einsum('bld,bld,bln->bldn', delta, u, Bm)
            shifted = jnp.concatenate([dA[:, 1:], jnp.zeros_like(dA[:, :1])], axis=1)
            e = jnp.exp(jnp.flip(jnp.cumsum(jnp.flip(shifted, axis=1), axis=1), axis=1))
            x = jnp.cumsum(dB_u * e, axis=1) / (e + 1e-12)
            y = jnp.einsum('bldn,bln->bld', x, Cm)
            return y + u * Dv
        key = jax.random.key(seed)
        ks = jax.random.split(key, 6)
        s = 0.02
        return {'x': jax.random.normal(ks[0], (B, L, D_MODEL), jnp.float32), 'W_in': jax.random.normal(ks[1], (D_MODEL, 2 * D_INNER), jnp.float32) * s, 'conv_k': jax.random.normal(ks[2], (K, D_INNER), jnp.float32) * s, 'conv_b': jnp.zeros((D_INNER,), jnp.float32), 'W_x': jax.random.normal(ks[3], (D_INNER, DT_RANK + 2 * N_STATE), jnp.float32) * s, 'W_dt': jax.random.normal(ks[4], (DT_RANK, D_INNER), jnp.float32) * s, 'b_dt': jnp.zeros((D_INNER,), jnp.float32), 'A_log': jnp.log(jnp.tile(jnp.arange(1, N_STATE + 1, dtype=jnp.float32)[None, :], (D_INNER, 1))), 'D_param': jnp.ones((D_INNER,), jnp.float32), 'W_out': jax.random.normal(ks[5], (D_INNER, D_MODEL), jnp.float32) * s}
    _L0_attn_all = _L0_attn_setup()
    _L0_attn_in = {k: v for k, v in _L0_attn_all.items() if k in ('W_in', 'conv_k', 'conv_b', 'W_x', 'W_dt', 'b_dt', 'A_log', 'D_param', 'W_out')}
    del _L0_attn_all

    def _L0_ffn_setup():
        import jax, jax.numpy as jnp
        import numpy as np
        B, T, IN_DIM = (64, 64, 64)
        HID, OUT_DIM = (128, 64)
        N_LAYERS, N_EXPERTS, N_SHARED = (2, 16, 1)
        key = jax.random.key(seed)
        ks = jax.random.split(key, 10)
        s = 0.02
        x = jax.random.normal(ks[0], (B, T, IN_DIM), dtype=jnp.float32)
        route_id = jax.random.randint(ks[1], (B,), 0, N_EXPERTS)
        Wi = jax.random.normal(ks[2], (HID, IN_DIM), dtype=jnp.float32) * s
        bi = jnp.zeros((HID,), dtype=jnp.float32)
        Wr = jax.random.normal(ks[3], (N_LAYERS, N_EXPERTS, HID, HID), dtype=jnp.float32) * s
        br = jax.random.normal(ks[4], (N_LAYERS, N_EXPERTS, HID), dtype=jnp.float32) * s
        Ws = jax.random.normal(ks[5], (N_LAYERS, N_SHARED, HID, HID), dtype=jnp.float32) * s
        bs = jax.random.normal(ks[6], (N_LAYERS, N_SHARED, HID), dtype=jnp.float32) * s
        Wo = jax.random.normal(ks[7], (OUT_DIM, HID), dtype=jnp.float32) * s
        bo = jnp.zeros((OUT_DIM,), dtype=jnp.float32)
        return {'x': x, 'route_id': route_id, 'Wi': Wi, 'bi': bi, 'Wr': Wr, 'br': br, 'Ws': Ws, 'bs': bs, 'Wo': Wo, 'bo': bo}
    _L0_ffn_all = _L0_ffn_setup()
    _L0_ffn_in = {k: v for k, v in _L0_ffn_all.items() if k in ('route_id', 'Wi', 'bi', 'Wr', 'br', 'Ws', 'bs', 'Wo', 'bo')}
    del _L0_ffn_all
    return {'x': x, 'L0_tok_W': _L0_tok_in['W'], 'L0_attn_W_in': _L0_attn_in['W_in'], 'L0_attn_conv_k': _L0_attn_in['conv_k'], 'L0_attn_conv_b': _L0_attn_in['conv_b'], 'L0_attn_W_x': _L0_attn_in['W_x'], 'L0_attn_W_dt': _L0_attn_in['W_dt'], 'L0_attn_b_dt': _L0_attn_in['b_dt'], 'L0_attn_A_log': _L0_attn_in['A_log'], 'L0_attn_D_param': _L0_attn_in['D_param'], 'L0_attn_W_out': _L0_attn_in['W_out'], 'L0_ffn_route_id': _L0_ffn_in['route_id'], 'L0_ffn_Wi': _L0_ffn_in['Wi'], 'L0_ffn_bi': _L0_ffn_in['bi'], 'L0_ffn_Wr': _L0_ffn_in['Wr'], 'L0_ffn_br': _L0_ffn_in['br'], 'L0_ffn_Ws': _L0_ffn_in['Ws'], 'L0_ffn_bs': _L0_ffn_in['bs'], 'L0_ffn_Wo': _L0_ffn_in['Wo'], 'L0_ffn_bo': _L0_ffn_in['bo']}

def reference(x, L0_tok_W, L0_attn_W_in, L0_attn_conv_k, L0_attn_conv_b, L0_attn_W_x, L0_attn_W_dt, L0_attn_b_dt, L0_attn_A_log, L0_attn_D_param, L0_attn_W_out, L0_ffn_route_id, L0_ffn_Wi, L0_ffn_bi, L0_ffn_Wr, L0_ffn_br, L0_ffn_Ws, L0_ffn_bs, L0_ffn_Wo, L0_ffn_bo):
    import jax
    import jax.numpy as jnp

    def _L0_tok_ref(x, W):
        import jax, jax.numpy as jnp
        import numpy as np
        PATCH_LEN = 16
        STRIDE = 8
        PAD = 8
        B, C, T, V = x.shape
        xp = jnp.pad(x, ((0, 0), (0, 0), (0, PAD), (0, 0)), mode='edge')
        Tp = T + PAD
        N = (Tp - PATCH_LEN) // STRIDE + 1
        idx = jnp.arange(N)[:, None] * STRIDE + jnp.arange(PATCH_LEN)[None, :]
        patches = xp[:, :, idx, :]
        patches = jnp.transpose(patches, (0, 4, 2, 3, 1))
        xf = jnp.fft.rfft(patches, axis=-2, norm='ortho')
        F = xf.shape[-2]
        x_real = xf.real.reshape(B, V, N, F * C)
        x_imag = xf.imag.reshape(B, V, N, F * C)
        x_emb = jnp.concatenate([x_real, x_imag], axis=-1)
        x_emb = x_emb @ W.T
        return x_emb.reshape(B, V * N, -1)

    def _L0_attn_ref(x, W_in, conv_k, conv_b, W_x, W_dt, b_dt, A_log, D_param, W_out):
        import jax, jax.numpy as jnp
        import numpy as np
        D_MODEL = 64
        D_INNER = 128
        N_STATE = 64
        DT_RANK = 16
        K = 4
        B, L = (2, 256)

        def _selective_scan(u, delta, A, Bm, Cm, Dv):
            dA = jnp.einsum('bld,dn->bldn', delta, A)
            dB_u = jnp.einsum('bld,bld,bln->bldn', delta, u, Bm)
            shifted = jnp.concatenate([dA[:, 1:], jnp.zeros_like(dA[:, :1])], axis=1)
            e = jnp.exp(jnp.flip(jnp.cumsum(jnp.flip(shifted, axis=1), axis=1), axis=1))
            x = jnp.cumsum(dB_u * e, axis=1) / (e + 1e-12)
            y = jnp.einsum('bldn,bln->bld', x, Cm)
            return y + u * Dv
        x_and_res = x @ W_in
        x_int, res = jnp.split(x_and_res, 2, axis=-1)
        xp = jnp.pad(x_int, ((0, 0), (K - 1, 0), (0, 0)))
        xc = jax.lax.conv_general_dilated(xp, conv_k[:, None, :], window_strides=(1,), padding='VALID', dimension_numbers=('NWC', 'WIO', 'NWC'), feature_group_count=D_INNER) + conv_b
        xc = jax.nn.swish(xc)
        x_dbl = xc @ W_x
        dl, Bm, Cm = jnp.split(x_dbl, [DT_RANK, DT_RANK + N_STATE], axis=-1)
        delta = jax.nn.softplus(dl @ W_dt + b_dt)
        A = -jnp.exp(A_log)
        y = _selective_scan(xc, delta, A, Bm, Cm, D_param)
        y = y * jax.nn.swish(res)
        return y @ W_out

    def _L0_ffn_ref(x, route_id, Wi, bi, Wr, br, Ws, bs, Wo, bo):
        import jax, jax.numpy as jnp
        import numpy as np
        B, T, IN_DIM = (64, 64, 64)
        HID, OUT_DIM = (128, 64)
        N_LAYERS, N_EXPERTS, N_SHARED = (2, 16, 1)
        flat = x.reshape(-1, x.shape[-1])
        n_tok = flat.shape[0]
        route = jnp.repeat(route_id, n_tok // route_id.shape[0])
        h = jax.nn.relu(flat @ Wi.T + bi)
        n_layers, n_experts = (Wr.shape[0], Wr.shape[1])
        for l in range(n_layers):
            shared = (jnp.einsum('nd,shd->snh', h, Ws[l]) + bs[l][:, None, :]).mean(axis=0)
            routed = jnp.zeros_like(h)
            for e in range(n_experts):
                ye = h @ Wr[l, e].T + br[l, e]
                routed = routed + jnp.where((route == e)[:, None], ye, 0.0)
            h = jax.nn.relu(shared + routed + h)
        out = h @ Wo.T + bo
        return out.reshape(*x.shape[:-1], out.shape[-1])
    h = _L0_tok_ref(x, L0_tok_W)
    h = h + _L0_attn_ref(_layernorm(h, axis=-1), L0_attn_W_in, L0_attn_conv_k, L0_attn_conv_b, L0_attn_W_x, L0_attn_W_dt, L0_attn_b_dt, L0_attn_A_log, L0_attn_D_param, L0_attn_W_out)
    h = h + _L0_ffn_ref(_layernorm(h, axis=-1), L0_ffn_route_id, L0_ffn_Wi, L0_ffn_bi, L0_ffn_Wr, L0_ffn_br, L0_ffn_Ws, L0_ffn_bs, L0_ffn_Wo, L0_ffn_bo)
    return h

_drawn_inputs = setup_inputs


def setup_inputs(seed=0):
    import zlib

    import numpy as np

    out = dict(_drawn_inputs(seed))
    spreads = {'L0_attn_conv_b': (0.0, 0.8),
     'L0_attn_b_dt': (0.0, 0.8),
     'L0_attn_D_param': (1.0, 0.6),
     'L0_ffn_bi': (0.0, 0.504),
     'L0_ffn_bo': (0.0, 0.1)}
    factors = {'L0_attn_W_in': 8.0,
     'L0_attn_conv_k': 8.0,
     'L0_attn_W_x': 8.0,
     'L0_attn_W_dt': 8.0,
     'L0_attn_A_log': 8.0,
     'L0_attn_W_out': 8.0,
     'L0_ffn_Wr': 3.408,
     'L0_ffn_br': 16.041,
     'L0_ffn_Ws': 3.429,
     'L0_ffn_bs': 15.463,
     'L0_ffn_Wi': 2.717}
    for name, (base, spread) in spreads.items():
        noise = np.random.default_rng([zlib.crc32(name.encode()), seed]).standard_normal(out[name].shape)
        drawn = base * np.exp(spread * noise) if base else spread * noise
        out[name] = jnp.asarray(drawn.astype(out[name].dtype))
    for name, factor in factors.items():
        out[name] = (out[name] * factor).astype(out[name].dtype)
    return out
```

```python
import concourse.bass as bass
from concourse import mybir
from contextlib import ExitStack


B, CH, T, V = 2, 64, 128, 64
PATCH, STRIDE = 16, 8
NP = T // STRIDE
L = V * NP
DM = 64
DI = 128
NS = 64
RK = 16
KC = 4
HID, NE, NL = 128, 16, 2
NG = 64
GT = B * L // NG
GB = NG // B
NF = PATCH // 2 + 1
RIF = 2 * NF
TL = 8
LR = L - TL
LN_EPS = 1e-5
E_EPS = 1e-12
ZERO_EXP = -110.0

C_ID, C_CC, C_IC, C_DFT, C_IOTA = 0, 128, 256, 384, 400
C_ALL = 401


def tower(nc, x, tok_w, w_in, conv_k, conv_b, w_x, w_dt, b_dt, a_log, d_par, w_out,
          route, wi, bi, wr, br, ws, bs, wo, bo, const, out):
    F32, I32 = mybir.dt.float32, mybir.dt.int32
    ALU, ACT, AX = mybir.AluOpType, mybir.ActivationFunctionType, mybir.AxisListType

    ctx = ExitStack()
    with ctx:
        def sb(name, shape, dt=F32):
            return ctx.enter_context(nc.sbuf_tensor(name, shape, dt))

        def bc(ap, shape):
            return ap.broadcast_to(shape)

        def sem(name):
            return ctx.enter_context(nc.semaphore(name))

        cst = sb("cst", [128, C_ALL])
        xs = sb("xs", [128, B, NP, 4 * V])
        xlast = sb("xlast", [128, B, V])
        wt = sb("wt", [RIF, DM, CH])
        weff = sb("weff", [128, 4, 2, DM])
        w_in2 = sb("w_in2", [128, 2 * DI])
        taps = sb("taps", [128, 2, DI])
        w_conv = sb("w_conv", [128, 2, DI])
        cb = sb("cb", [128, 1])
        ncb = sb("ncb", [128, 1])
        wx = sb("wx", [DI, RK + 2 * NS])
        wxT = sb("wxT", [RK, DI])
        wdt = sb("wdt", [RK, DI])
        wdelta = sb("wdelta", [DI, DI])
        bdt = sb("bdt", [128, 1])
        nbdt = sb("nbdt", [128, 1])
        alog = sb("alog", [128, NS])
        A = sb("A", [128, NS])
        amax = sb("amax", [128, 1])
        dpar = sb("dpar", [128, 1])
        wout = sb("wout", [DI, 2, DM])
        wmean = sb("wmean", [DI, 1])
        rid = sb("rid", [1, NG], I32)
        ridb = sb("ridb", [NE, NG], I32)
        onehot = sb("onehot", [NE + 1, NG])
        wi2 = sb("wi2", [HID, 2, DM])
        wiT = sb("wiT", [128, HID])
        bib = sb("bib", [HID, 1])
        brs = sb("brs", [NE + 1, NL, HID])
        wsh = sb("wsh", [HID, NL, HID])
        wrn = sb("wrn", [HID, NL, NE, HID])
        wexp = sb("wexp", [HID, NE, NL, HID])
        wsel = sb("wsel", [HID, NG, NL, HID])
        won = sb("won", [DM, HID])
        woT = sb("woT", [HID, DM])
        resid = sb("resid", [DM + 1, DM])
        ones = sb("ones", [128, 128])
        onecol = sb("onecol", [128, 1])
        ceps = sb("ceps", [128, 1])
        ones64 = sb("ones64", [128, 128])
        gbuf = sb("gbuf", [128, LR])
        seg = sb("seg", [128, NS, TL])
        tok = [sb(f"tok{b}", [128, L]) for b in range(B)]
        xn = [sb(f"xn{b}", [128, L + KC]) for b in range(B)]
        u = [sb(f"u{b}", [128, L]) for b in range(B)]
        gate = [sb(f"gate{b}", [128, L]) for b in range(B)]
        h2 = [sb(f"h2{b}", [DM + 1, L]) for b in range(B)]
        carry = sb("carry", [128, B, NS])
        ytail = sb("ytail", [128, B, TL])
        safe = sb("safe", [128, B])
        count = sb("count", [1, B], I32)
        wcur = sb("wcur", [128, 2])
        acur = sb("acur", [128, 1])
        scr = xs[:, :, :, :].rearrange("p b (k s) c -> p b k (s c)", k=4)

        def slot(b, k):
            return scr[:, b, k, :]

        ps = [[ctx.enter_context(nc.psum_tensor(f"ps{b}{p}", [128, L], F32)) for p in range(2)]
              for b in range(B)]

        def weff_to(h, odd):
            return weff[64 * h:64 * h + 64, :, :, :].rearrange("p q a (j e) -> p e a q j", e=2)[:, odd]

        def weff_from(h, odd):
            return ps[0][0][64 * odd:64 * odd + 64, 0:512].rearrange("p (j a h q) -> p h a q j", a=2, h=2, q=4)[:, h]

        names_load = ["s_const", "s_tokw", "s_attw", "s_convw", "s_ffnw", "s_route", "s_x00", "s_x01",
                      "s_x10", "s_x11", "s_ws", "s_wr0", "s_wr1", "s_wr2", "s_wr3"]
        ld = {n: sem(n) for n in names_load}
        s_weff_mm, s_weff = sem("s_weff_mm"), sem("s_weff")
        s_set, s_setx = sem("s_set"), sem("s_setx")
        s_wtr, s_wtrc = sem("s_wtr"), sem("s_wtrc")
        s_wd, s_wdc = sem("s_wd"), sem("s_wdc")
        s_prep = sem("s_prep")
        s_A = sem("s_A")
        s_tok, s_tokA, s_tokB = sem("s_tok"), sem("s_tokA"), sem("s_tokB")
        s_cc, s_sq, s_var, s_ln, s_rstd, s_xn = (sem(n) for n in
                                                 ["s_cc", "s_sq", "s_var", "s_ln", "s_rstd", "s_xn"])
        s_xc, s_res, s_exc, s_eres, s_u, s_gate = (sem(n) for n in
                                                   ["s_xc", "s_res", "s_exc", "s_eres", "s_u", "s_gate"])
        s_dz, s_sp, s_spl, s_dl, s_du, s_R = (sem(n) for n in
                                              ["s_dz", "s_sp", "s_spl", "s_dl", "s_du", "s_R"])
        s_safe, s_cnt, s_flag = sem("s_safe"), sem("s_cnt"), sem("s_flag")
        s_B0, s_C0, s_tl = sem("s_B0"), sem("s_C0"), sem("s_tl")
        s_w, s_E, s_E1, s_Eu, s_y0, s_argT, s_ET, s_yg = (sem(n) for n in
            ["s_w", "s_E", "s_E1", "s_Eu", "s_y0", "s_argT", "s_ET", "s_yg"])
        s_z2, s_h2, s_sq2, s_var2, s_ln2, s_rstd2, s_xn2 = (sem(n) for n in
            ["s_z2", "s_h2", "s_sq2", "s_var2", "s_ln2", "s_rstd2", "s_xn2"])
        s_wi, s_h1, s_l1, s_r1, s_l2, s_r2, s_fin, s_oc, s_out = (sem(n) for n in
            ["s_wi", "s_h1", "s_l1", "s_r1", "s_l2", "s_r2", "s_fin", "s_oc", "s_out"])
        s_wadd, s_ex, s_exc4, s_sel = sem("s_wadd"), sem("s_ex"), sem("s_exc4"), sem("s_sel")
        g_cp = [sem(f"g_cp{b}") for b in range(B)]
        g_E = [sem(f"g_E{b}") for b in range(B)]
        g_B = [sem(f"g_B{b}") for b in range(B)]
        g_w = [sem(f"g_w{b}") for b in range(B)]
        g_C = [sem(f"g_C{b}") for b in range(B)]
        g_v = [sem(f"g_v{b}") for b in range(B)]
        g_m = [sem(f"g_m{b}") for b in range(B)]
        g_y = [sem(f"g_y{b}") for b in range(B)]
        s_v, s_a, s_p = sem("s_v"), sem("s_a"), sem("s_p")

        ident = cst[:, C_ID:C_ID + 128]
        c_cc = cst[:, C_CC:C_CC + 128]
        c_ic = cst[:, C_IC:C_IC + 128]

        x_v = x.rearrange("b c (s h r) v -> b h c s (r v)", h=2, r=4)

        K0, K1, K2, K3 = range(4)

        block = ctx.enter_context(nc.Block())

        @block.sync
        def _(sp):
            sp.dma_start(wt[:, :, :], tok_w.rearrange("o (r c) -> r o c", r=RIF)).then_inc(ld["s_tokw"], 16)
            for b in range(B):
                for k in range(2):
                    sp.dma_start(xs[0:CH, b, 8 * k:8 * k + 8, :], x_v[b, 0, :, 8 * k:8 * k + 8, :]
                                 ).then_inc(ld[f"s_x{b}{k}"], 16)
                sp.dma_start(xlast[0:CH, b, :], x[b, :, T - 1, :]).then_inc(ld[f"s_x{b}1"], 16)
                if b == 0:
                    sp.dma_start(wsh[:, :, :], ws.rearrange("l s h d -> h (l s) d")).then_inc(ld["s_ws"], 16)
            for k in range(4):
                l, e = k // 2, NE // 2 * (k % 2)
                sp.dma_start(wrn[:, l, e:e + NE // 2, :], wr[l, e:e + NE // 2, :, :].rearrange("e h d -> h e d")
                             ).then_inc(ld[f"s_wr{k}"], 16)
            for b in range(B):
                sp.wait_ge(s_oc, b + 1)
                sp.dma_start(out[b, :, :].rearrange("(p j) o -> p (j o)", j=8), slot(b, K0)[:, 0:8 * DM]
                             ).then_inc(s_out, 16)
            sp.wait_ge(s_out, 16 * B)

        @block.gpsimd
        def _(pool):
            def load(name, to, src):
                pool.dma_start(to, src).then_inc(ld[name], 16)
            load("s_attw", wx[:, :], w_x)
            load("s_attw", wdt[:, :], w_dt)
            load("s_attw", bdt[:, :], b_dt.rearrange("(p a) -> p a", a=1))
            load("s_attw", alog[:, :], a_log)
            load("s_attw", dpar[:, :], d_par.rearrange("(p a) -> p a", a=1))
            load("s_attw", wout[:, 0, :], w_out)
            load("s_ffnw", wi2[:, 0, :], wi)
            load("s_ffnw", wi2[:, 1, :], wi)
            load("s_ffnw", bib[:, :], bi.rearrange("(p a) -> p a", a=1))
            load("s_ffnw", brs[0:NE, :, :], br.rearrange("l e h -> e l h"))
            load("s_ffnw", brs[NE:NE + 1, :, :], bs.rearrange("l s h -> s l h"))
            load("s_ffnw", won[:, :], wo)
            load("s_ffnw", resid[DM:DM + 1, :], bo.rearrange("(a n) -> a n", a=1))
            load("s_route", rid[:, :], route.rearrange("(a n) -> a n", a=1))
            load("s_route", ridb[:, :], route.rearrange("(a n) -> a n", a=1).broadcast_to([NE, NG]))
            pool.memset(seg[:, :, :], 1.0).then_inc(s_p, 1)
            pool.wait_ge(s_p, 1)
            pool.memset(seg[:, :, 0:1], 0.0).then_inc(s_setx, 1)
            pool.memset(carry[:, :, :], 0.0).then_inc(s_setx, 1)
            pool.wait_ge(ld["s_ws"], 16)
            pool.wait_ge(ld["s_const"], 16)
            pool.tensor_tensor(wsh[:, :, :], wsh[:, :, :], bc(ident.unsqueeze(1), [HID, NL, HID]), ALU.add
                               ).then_inc(s_p, 1)
            pool.wait_ge(s_p, 2)
            for k in range(4):
                l, e = k // 2, NE // 2 * (k % 2)
                w = wrn[:, l, e:e + NE // 2, :]
                pool.wait_ge(ld[f"s_wr{k}"], 16)
                pool.tensor_tensor(w, w, bc(wsh[:, l:l + 1, :], [HID, NE // 2, HID]), ALU.add).then_inc(s_wadd, 1)
            pool.wait_ge(s_exc4, 4)
            pool.wait_ge(ld["s_route"], 32)
            for b in range(B):
                with pool.Fori(b * GB, (b + 1) * GB) as g:
                    e = pool.value_load(rid[0:1, bass.ds(g, 1)], min_val=0, max_val=NE - 1)
                    pool.tensor_copy(wsel[:, bass.ds(g, 1), :, :], wexp[:, bass.ds(e, 1), :, :]).then_inc(s_sel, 1)

        @block.scalar
        def _(act):
            for to, src, name in (
                    [(cst[:, :], const, "s_const")]
                    + [(xs[CH:128, 0, 8 * k:8 * k + 8, :], x_v[0, 1, :, 8 * k:8 * k + 8, :], f"s_x0{k}") for k in range(2)]
                    + [(xlast[CH:128, 0, :], x[0, :, T - 1, :], "s_x01")]
                    + [(w_in2[64 * k:64 * k + 64, :], w_in, "s_convw") for k in range(2)]
                    + [(taps[64 * h:64 * h + 64, k, :], conv_k[3 - 2 * k - h:4 - 2 * k - h, :].broadcast_to([64, DI]), "s_convw")
                       for h in range(2) for k in range(2)]
                    + [(cb[:, :], conv_b.rearrange("(p a) -> p a", a=1), "s_convw")]
                    + [(xs[CH:128, 1, 8 * k:8 * k + 8, :], x_v[1, 1, :, 8 * k:8 * k + 8, :], f"s_x1{k}") for k in range(2)]
                    + [(xlast[CH:128, 1, :], x[1, :, T - 1, :], "s_x11")]):
                act.dma_start(to, src).then_inc(ld[name], 16)
            steps = [0]

            def step(ins):
                ins.then_inc(s_a, 1)
                steps[0] += 1
                act.wait_ge(s_a, steps[0])

            def weights():
                act.wait_ge(s_weff_mm, 1)
                for h in range(2):
                    act.activation(weff_to(h, 0), weff_from(h, 0), ACT.Copy).then_inc(s_weff, 1)
                act.wait_ge(ld["s_attw"], 96)
                step(act.activation(A[:, :], alog[:, :], ACT.Exp))
                act.activation(A[:, :], A[:, :], ACT.Copy, scale=-1.0).then_inc(s_A, 1)

            def tokens(b):
                act.wait_ge(s_tok, b + 1)
                act.activation(tok[b][0:64, :].rearrange("p (v n) -> p n v", n=NP),
                               ps[b][0][0:64, :].rearrange("p (n v) -> p n v", v=V), ACT.Copy).then_inc(s_tokA, 1)

            def square(b):
                act.wait_ge(s_cc, b + 1)
                act.activation(slot(b, K0), ps[b][1][:, :], ACT.Square).then_inc(s_sq, 1)

            def rstd(b):
                act.wait_ge(s_var, b + 1)
                act.activation(slot(b, K1), ps[b][0][:, :], ACT.Ln, bias=ceps[:, 0:1]).then_inc(s_ln, 1)
                act.wait_ge(s_ln, b + 1)
                act.activation(slot(b, K1), slot(b, K1), ACT.Exp, scale=-0.5).then_inc(s_rstd, 1)

            def exp_conv(b):
                act.wait_ge(s_prep, 1)
                act.wait_ge(s_xc, b + 1)
                act.activation(slot(b, K0), ps[b][1][:, :], ACT.Exp, bias=ncb[:, 0:1], scale=-1.0).then_inc(s_exc, 1)

            def exp_res(b):
                act.wait_ge(s_res, b + 1)
                act.activation(slot(b, K2), ps[b][0][:, :], ACT.Exp, scale=-1.0).then_inc(s_eres, 1)

            def softplus(b):
                act.wait_ge(s_u, b + 1)
                act.wait_ge(s_dz, b + 1)
                step(act.activation(slot(b, K1), ps[b][1][:, :], ACT.Abs, bias=bdt[:, 0:1]))
                step(act.activation(slot(b, K1), slot(b, K1), ACT.Exp, scale=-1.0))
                act.activation(slot(b, K1), slot(b, K1), ACT.Ln, bias=1.0).then_inc(s_spl, 1)

            def decay(b):
                act.wait_ge(s_R, b + 1)
                act.activation(slot(b, K1)[:, 0:LR], slot(b, K3)[:, 0:LR], ACT.Exp, scale=A[:, 0:1]).then_inc(s_E, 1)
                act.wait_ge(s_argT, b + 1)
                act.activation(xn[b][:, 0:NS * TL], xn[b][:, 0:NS * TL], ACT.Exp).then_inc(s_ET, 1)
                act.wait_ge(s_cnt, b + 1)
                act.activation(count[0:1, b:b + 1], ps[b][1][0:1, LR + 4:LR + 5], ACT.Copy).then_inc(s_flag, 1)

            def general(b):
                act.wait_ge(s_flag, b + 1)
                act.wait_ge(s_y0, b + 1)
                lanes = act.value_load(count[0:1, b:b + 1], min_val=0, max_val=128)
                with act.If(lanes < 128):
                    with act.Fori(1, NS) as n:
                        act.wait_ge(g_y[b], n)
                        act.activation(wcur[:, 0:1], wx[:, bass.ds(n + RK, 1)], ACT.Copy).then_inc(g_cp[b], 1)
                        act.activation(wcur[:, 1:2], wx[:, bass.ds(n + RK + NS, 1)], ACT.Copy).then_inc(g_cp[b], 1)
                        act.activation(acur[:, 0:1], A[:, bass.ds(n, 1)], ACT.Copy).then_inc(g_cp[b], 1)
                        act.wait_ge(g_cp[b], n * 3)
                        act.activation(slot(b, K1)[:, 0:LR], slot(b, K3)[:, 0:LR], ACT.Exp, scale=acur[:, 0:1]
                                       ).then_inc(g_E[b], 1)

            def norm2(b):
                act.wait_ge(s_z2, b + 1)
                act.activation(slot(b, K0)[64:128, :], ps[b][1][64:128, :], ACT.Square).then_inc(s_sq2, 1)
                act.activation(h2[b][0:DM, :], ps[b][1][0:DM, :], ACT.Copy).then_inc(s_h2, 1)
                act.wait_ge(s_var2, b + 1)
                act.activation(slot(b, K1)[64:128, :], ps[b][0][64:128, :], ACT.Ln, bias=ceps[64:128, 0:1]
                               ).then_inc(s_ln2, 1)
                act.wait_ge(s_ln2, b + 1)
                act.activation(slot(b, K1)[64:128, :], slot(b, K1)[64:128, :], ACT.Exp, scale=-0.5
                               ).then_inc(s_rstd2, 1)

            def relu_in(b):
                act.wait_ge(s_wi, b + 1)
                act.activation(slot(b, K0), ps[b][1][:, :], ACT.Relu, bias=bib[:, 0:1]).then_inc(s_h1, 1)

            def relu_1(b):
                act.wait_ge(s_l1, b + 1)
                act.activation(slot(b, K1), ps[b][0][:, :], ACT.Relu).then_inc(s_r1, 1)

            def relu_2(b):
                act.wait_ge(s_l2, b + 1)
                act.activation(slot(b, K2), ps[b][1][:, :], ACT.Relu).then_inc(s_r2, 1)

            def out_copy(b):
                act.wait_ge(s_fin, b + 1)
                act.activation(slot(b, K0)[:, 0:8 * DM], ps[b][0][:, 0:8 * DM], ACT.Copy).then_inc(s_oc, 1)

            def experts(k):
                l, e = k // 2, NE // 2 * (k % 2)
                act.wait_ge(s_ex, k + 1)
                act.activation(wexp[:, e:e + NE // 2, l, :], ps[1][1 - k % 2][:, :].rearrange("p (e h) -> p e h", h=HID),
                               ACT.Copy).then_inc(s_exc4, 1)

            weights()
            tokens(0)
            square(0)
            act.wait_ge(s_set, 1)
            rstd(0)
            tokens(1)
            exp_conv(0)
            exp_res(0)
            square(1)
            rstd(1)
            softplus(0)
            decay(0)
            exp_conv(1)
            exp_res(1)
            experts(0)
            experts(1)
            experts(2)
            experts(3)
            general(0)
            softplus(1)
            decay(1)
            norm2(0)
            act.wait_ge(ld["s_ffnw"], 112)
            relu_in(0)
            relu_1(0)
            general(1)
            relu_2(0)
            out_copy(0)
            norm2(1)
            relu_in(1)
            relu_1(1)
            relu_2(1)
            out_copy(1)

        @block.tensor
        def _(pe):
            mm = nc.tensor.matmul

            def halves(pair, lhsT, rhs, n=L, start=True, stop=True):
                for c in range(0, n, 512):
                    last = mm(pair[:, c:min(c + 512, n)], lhsT, rhs[:, c:min(c + 512, n)], start=start, stop=stop)
                return last

            def token_weights():
                pe.wait_ge(ld["s_tokw"], 16)
                pe.wait_ge(ld["s_const"], 16)
                for j in range(DM // 2):
                    last = mm(ps[0][0][:, 16 * j:16 * j + 16], wt[:, 2 * j:2 * j + 2, :],
                              cst[0:RIF, C_DFT:C_DFT + PATCH], start=True, stop=True)
                last.then_inc(s_weff_mm, 1)

            def tokens(b):
                if b == 0:
                    pe.wait_ge(s_weff, 4)
                else:
                    pe.wait_ge(s_prep, 1)
                for k in range(2):
                    pe.wait_ge(ld[f"s_x{b}{k}"], 32 + 32 * k)
                    for q in range(4):
                        mm(ps[b][0][:, 512 * k:512 * k + 512], weff[:, q, :, :],
                           xs[:, b, 8 * k:8 * k + 8, V * q:V * q + V], start=q == 0, stop=q == 3)
                for q in range(4):
                    last = mm(ps[b][1][:, 0:V], weff[:, q, :, :], xlast[:, b, :], start=q == 0, stop=q == 3)
                last.then_inc(s_tok, 1)

            def small_weights():
                pe.wait_ge(ld["s_attw"], 96)
                nc.tensor.transpose(ps[1][1][0:RK, 0:DI], wx[:, 0:RK], ident)
                pe.wait_ge(ld["s_ffnw"], 112)
                nc.tensor.transpose(ps[1][1][:, 128:128 + HID], wi2[:, :, :], ident)
                nc.tensor.transpose(ps[1][1][:, 256:256 + DM], won[:, :], cst[0:DM, C_ID:C_ID + DM]).then_inc(s_wtr, 1)
                pe.wait_ge(s_wtrc, 1)
                mm(ps[1][1][:, 512:512 + DI], wxT[:, :], wdt[:, :], start=True, stop=True).then_inc(s_wd, 1)

            def centered(b):
                pe.wait_ge(s_tokA, b + 1)
                pe.wait_ge(s_tokB, b + 1)
                halves(ps[b][1], c_cc, tok[b]).then_inc(s_cc, 1)

            def variance(b):
                pe.wait_ge(s_set, 1)
                pe.wait_ge(s_sq, b + 1)
                halves(ps[b][0], ones[:, :], slot(b, K0)).then_inc(s_var, 1)

            def conv(b):
                pe.wait_ge(s_prep, 1)
                pe.wait_ge(s_xn, b + 1)
                for c in range(0, L, 512):
                    mm(ps[b][1][:, c:c + 512], w_conv[:, 0, :], xn[b][:, c + 2:c + 514], start=True, stop=False)
                    last = mm(ps[b][1][:, c:c + 512], w_conv[:, 1, :], xn[b][:, c:c + 512], start=False, stop=True)
                last.then_inc(s_xc, 1)
                halves(ps[b][0], w_in2[0:64, DI:2 * DI], xn[b][0:64, 2:L + 2]).then_inc(s_res, 1)

            def delta(b):
                pe.wait_ge(s_u, b + 1)
                halves(ps[b][1], wdelta[:, :], u[b]).then_inc(s_dz, 1)

            def first_state(b):
                pe.wait_ge(s_gate, b + 1)
                halves(ps[b][0], bc(wx[:, RK:RK + 1], [DI, 128]), u[b], LR).then_inc(s_B0, 1)
                pe.wait_ge(s_dl, b + 1)
                halves(ps[b][1], bc(wx[:, RK + NS:RK + NS + 1], [DI, 128]), u[b], LR).then_inc(s_C0, 1)

            def safe_lanes(b):
                pe.wait_ge(s_safe, b + 1)
                mm(ps[b][1][0:1, LR + 4:LR + 5], safe[:, b:b + 1], onecol[:, :], start=True, stop=True).then_inc(s_cnt, 1)

            def tail(b):
                pe.wait_ge(s_w, b + 1)
                for t in range(TL):
                    last = mm(ps[b][0][:, 128 * t:128 * t + 128], bc(u[b][:, LR + t:LR + t + 1], [DI, 128]),
                              wx[:, RK:RK + 2 * NS], start=True, stop=True)
                last.then_inc(s_tl, 1)

            def general(b):
                pe.wait_ge(s_flag, b + 1)
                pe.wait_ge(s_y0, b + 1)
                lanes = pe.value_load(count[0:1, b:b + 1], min_val=0, max_val=128)
                with pe.If(lanes < 128):
                    with pe.Fori(1, NS) as n:
                        pe.wait_ge(g_cp[b], n * 3)
                        pe.wait_ge(g_y[b], n)
                        halves(ps[b][1], bc(wcur[:, 0:1], [DI, 128]), u[b], LR).then_inc(g_B[b], 1)
                        pe.wait_ge(g_w[b], n)
                        halves(ps[b][1], bc(wcur[:, 1:2], [DI, 128]), u[b], LR).then_inc(g_C[b], 1)

            def attention_out(b):
                pe.wait_ge(s_yg, b + 1)
                for c in range(0, L, 512):
                    mm(ps[b][1][:, c:c + 512], c_ic, tok[b][:, c:c + 512], start=True, stop=False)
                    last = mm(ps[b][1][:, c:c + 512], wout[:, :, :], slot(b, K1)[:, c:c + 512], start=False, stop=True)
                last.then_inc(s_z2, 1)

            def variance2(b):
                pe.wait_ge(s_sq2, b + 1)
                halves(ps[b][0], ones64[64:128, :], slot(b, K0)[64:128, :]).then_inc(s_var2, 1)

            def ffn_in(b):
                pe.wait_ge(s_h2, b + 1)
                pe.wait_ge(s_xn2, b + 1)
                halves(ps[b][1], wiT[64:128, :], slot(b, K2)[64:128, :]).then_inc(s_wi, 1)

            def ffn_layer(b, l):
                pair, h = (ps[b][0], slot(b, K0)) if l == 0 else (ps[b][1], slot(b, K1))
                if l == 0:
                    pe.wait_ge(s_h1, b + 1)
                    pe.wait_ge(s_sel, GB * (b + 1))
                else:
                    pe.wait_ge(s_r1, b + 1)
                per = 512 // GT
                for c in range(2):
                    g0 = b * GB + c * per
                    mm(pair[:, 512 * c:512 * c + 512], brs[:, l, :],
                       bc(onehot[:, g0:g0 + per].unsqueeze(2), [NE + 1, per, GT]), start=True, stop=False)
                    for k in range(per):
                        at = 512 * c + GT * k
                        last = mm(pair[:, at:at + GT], wsel[:, g0 + k, l, :], h[:, at:at + GT],
                                  start=False, stop=k == per - 1)
                last.then_inc(s_l1 if l == 0 else s_l2, 1)

            def ffn_out(b):
                pe.wait_ge(s_r2, b + 1)
                hv = slot(b, K2).rearrange("p (t j) -> p j t", j=8)
                rv = h2[b][:, :].rearrange("p (t j) -> p j t", j=8)
                for j in range(8):
                    mm(ps[b][0][:, DM * j:DM * j + DM], hv[:, j, :], woT[:, :], start=True, stop=False)
                    last = mm(ps[b][0][:, DM * j:DM * j + DM], rv[:, j, :], resid[:, :], start=False, stop=True)
                last.then_inc(s_fin, 1)

            def experts():
                for k in range(4):
                    l, e = k // 2, NE // 2 * (k % 2)
                    pe.wait_ge(s_wadd, k + 1)
                    if k >= 2:
                        pe.wait_ge(s_exc4, k - 1)
                    for i in range(NE // 2):
                        last = nc.tensor.transpose(ps[1][1 - k % 2][:, 128 * i:128 * i + 128], wrn[:, l, e + i, :], ident)
                    last.then_inc(s_ex, 1)

            token_weights()
            tokens(0)
            small_weights()
            centered(0)
            variance(0)
            tokens(1)
            conv(0)
            centered(1)
            variance(1)
            delta(0)
            first_state(0)
            conv(1)
            safe_lanes(0)
            tail(0)
            pe.wait_ge(s_gate, 2)
            pe.wait_ge(s_u, 2)
            experts()
            general(0)
            pe.wait_ge(s_exc4, 4)
            delta(1)
            first_state(1)
            safe_lanes(1)
            attention_out(0)
            variance2(0)
            ffn_in(0)
            tail(1)
            ffn_layer(0, 0)
            general(1)
            ffn_layer(0, 1)
            ffn_out(0)
            attention_out(1)
            variance2(1)
            ffn_in(1)
            ffn_layer(1, 0)
            ffn_layer(1, 1)
            ffn_out(1)

        @block.vector
        def _(dve):
            v = nc.vector
            steps = [0]

            def step(ins):
                ins.then_inc(s_v, 1)
                steps[0] += 1
                dve.wait_ge(s_v, steps[0])

            def constants():
                v.memset(onecol[:, :], 1.0)
                v.memset(ceps[:, :], LN_EPS)
                for b in range(B):
                    v.memset(xn[b][:, 0:KC], 0.0)
                    v.memset(h2[b][DM:DM + 1, :], 1.0)
                v.memset(onehot[:, :], 1.0)
                v.memset(ones64[:, :], 1.0 / 64)
                v.memset(ones[:, :], 1.0 / 128).then_inc(s_set, 1)

            def token_weights():
                dve.wait_ge(s_weff_mm, 1)
                for h in range(2):
                    v.tensor_copy(weff_to(h, 1), weff_from(h, 1)).then_inc(s_weff, 1)

            def small_weights():
                dve.wait_ge(ld["s_convw"], 112)
                v.tensor_tensor(w_conv[:, :, :], bc(w_in2[:, 0:DI].unsqueeze(1), [128, 2, DI]), taps[:, :, :], ALU.mult)
                v.tensor_scalar(ncb[:, :], cb[:, :], -1.0, None, ALU.mult)
                dve.wait_ge(s_wtr, 1)
                v.tensor_copy(wxT[:, :], ps[1][1][0:RK, 0:DI]).then_inc(s_wtrc, 1)
                v.tensor_copy(wiT[:, :], ps[1][1][:, 128:128 + HID])
                v.tensor_copy(woT[:, :], ps[1][1][:, 256:256 + DM])
                v.tensor_scalar(nbdt[:, :], bdt[:, :], -1.0, None, ALU.mult)
                step(v.reduce_sum(wmean[:, :], wout[:, 0, :], AX.X))
                v.memset(resid[0:DM, :], 0.0)
                step(v.tensor_scalar(wmean[:, :], wmean[:, :], 1.0 / DM, None, ALU.mult))
                v.tensor_scalar(wout[:, 1, :], wout[:, 0, :], wmean[:, 0:1], None, ALU.subtract)
                v.tensor_copy(resid[0:DM, :], cst[0:DM, C_ID:C_ID + DM])
                dve.wait_ge(s_A, 1)
                v.reduce_max(amax[:, :], A[:, 1:NS], AX.X)
                dve.wait_ge(ld["s_route"], 32)
                dve.wait_ge(s_set, 1)
                v.tensor_scalar(onehot[0:NE, :], ridb[:, :], cst[0:NE, C_IOTA:C_IOTA + 1], None, ALU.is_equal)
                dve.wait_ge(s_wd, 1)
                v.tensor_copy(wdelta[:, :], ps[1][1][:, 512:512 + DI]).then_inc(s_prep, 1)

            def tokens(b):
                dve.wait_ge(s_tok, b + 1)
                to = tok[b][64:128, :].rearrange("p (v n) -> p n v", n=NP)
                v.tensor_copy(to[:, 0:NP - 1, :], ps[b][0][64:128, V:L].rearrange("p (n v) -> p n v", v=V))
                v.tensor_copy(to[:, NP - 1, :], ps[b][1][64:128, 0:V]).then_inc(s_tokB, 1)

            def norm(b):
                dve.wait_ge(s_rstd, b + 1)
                v.tensor_tensor(xn[b][0:64, 2:L + 2], ps[b][1][0:64, :], slot(b, K1)[0:64, :], ALU.mult)
                v.tensor_tensor(xn[b][64:128, 3:L + 3], ps[b][1][64:128, :], slot(b, K1)[64:128, :], ALU.mult
                                ).then_inc(s_xn, 1)

            def swish_conv(b):
                dve.wait_ge(s_exc, b + 1)
                step(v.tensor_scalar(slot(b, K0), slot(b, K0), 1.0, None, ALU.add))
                step(v.reciprocal(slot(b, K1), slot(b, K0)))
                v.scalar_tensor_tensor(u[b][:, :], ps[b][1][:, :], cb[:, 0:1], slot(b, K1), ALU.add, ALU.mult
                                       ).then_inc(s_u, 1)

            def swish_res(b):
                dve.wait_ge(s_eres, b + 1)
                step(v.tensor_scalar(slot(b, K2), slot(b, K2), 1.0, None, ALU.add))
                step(v.reciprocal(slot(b, K2), slot(b, K2)))
                v.tensor_tensor(gate[b][:, :], ps[b][0][:, :], slot(b, K2), ALU.mult).then_inc(s_gate, 1)

            def steps_sum(b):
                dve.wait_ge(s_spl, b + 1)
                v.scalar_tensor_tensor(slot(b, K0), ps[b][1][:, :], nbdt[:, 0:1], slot(b, K1), ALU.max, ALU.add
                                       ).then_inc(s_dl, 1)
                dve.wait_ge(s_dl, b + 1)
                dve.wait_ge(s_gate, b + 1)
                v.memset(slot(b, K3)[:, L - 1:L], 0.0)
                step(v.tensor_tensor_scan(slot(b, K3)[:, 0:L - 1][:, ::-1], slot(b, K0)[:, 1:L][:, ::-1],
                                          bc(bdt[:, 0:1], [128, L - 1]), 0.0, ALU.add, ALU.add))
                v.scalar_tensor_tensor(slot(b, K2), slot(b, K0), bdt[:, 0:1], u[b][:, :], ALU.add, ALU.mult
                                       ).then_inc(s_R, 1)
                step(v.tensor_scalar(safe[:, b:b + 1], amax[:, 0:1], slot(b, K3)[:, LR - 1:LR], None, ALU.mult))
                v.tensor_scalar(safe[:, b:b + 1], safe[:, b:b + 1], ZERO_EXP, None, ALU.is_le).then_inc(s_safe, 1)
                v.tensor_tensor(xn[b][:, 0:NS * TL].rearrange("p (n t) -> p n t", t=TL),
                                bc(slot(b, K3)[:, LR:L].unsqueeze(1), [128, NS, TL]),
                                bc(A[:, :].unsqueeze(2), [128, NS, TL]), ALU.mult).then_inc(s_argT, 1)

            def first_state(b):
                dve.wait_ge(s_B0, b + 1)
                dve.wait_ge(s_R, b + 1)
                w = slot(b, K0)[:, 0:LR]
                E = slot(b, K1)[:, 0:LR]
                v.tensor_tensor(w, ps[b][0][:, 0:LR], slot(b, K2)[:, 0:LR], ALU.mult).then_inc(s_w, 1)
                dve.wait_ge(s_w, b + 1)
                dve.wait_ge(s_E, b + 1)
                step(v.tensor_tensor(w, w, E, ALU.mult))
                step(v.tensor_scalar(E, E, E_EPS, None, ALU.add))
                step(v.tensor_tensor_scan(w, bc(onecol[:, 0:1], [128, LR]), w, 0.0, ALU.mult, ALU.add))
                dve.wait_ge(s_setx, 2)
                v.tensor_copy(carry[:, b, 0:1], slot(b, K0)[:, LR - 1:LR])
                step(v.reciprocal(E, E))
                step(v.tensor_tensor(w, w, E, ALU.mult))
                dve.wait_ge(s_C0, b + 1)
                v.tensor_tensor(w, w, ps[b][1][:, 0:LR], ALU.mult).then_inc(s_y0, 1)
                dve.wait_ge(s_y0, b + 1)

            def general(b):
                dve.wait_ge(s_flag, b + 1)
                lanes = dve.value_load(count[0:1, b:b + 1], min_val=0, max_val=128)
                y, E = slot(b, K0)[:, 0:LR], slot(b, K1)[:, 0:LR]
                with dve.If(lanes < 128):
                    v.memset(gbuf[:, 0:1], 0.0).then_inc(g_y[b], 1)
                    dve.wait_ge(g_y[b], 1)
                    with dve.Fori(1, NS) as n:
                        dve.wait_ge(g_B[b], n)
                        v.tensor_tensor(gbuf[:, :], ps[b][1][:, 0:LR], slot(b, K2)[:, 0:LR], ALU.mult
                                        ).then_inc(g_w[b], 1)
                        dve.wait_ge(g_w[b], n)
                        dve.wait_ge(g_E[b], n)
                        v.tensor_tensor(gbuf[:, :], gbuf[:, :], E, ALU.mult).then_inc(g_v[b], 1)
                        dve.wait_ge(g_v[b], n * 6 - 5)
                        v.tensor_scalar(E, E, E_EPS, None, ALU.add).then_inc(g_v[b], 1)
                        v.tensor_tensor_scan(gbuf[:, :], bc(onecol[:, 0:1], [128, LR]), gbuf[:, :], 0.0,
                                             ALU.mult, ALU.add).then_inc(g_v[b], 1)
                        dve.wait_ge(g_v[b], n * 6 - 3)
                        v.tensor_copy(carry[:, b, bass.ds(n, 1)], gbuf[:, LR - 1:LR]).then_inc(g_v[b], 1)
                        v.reciprocal(E, E).then_inc(g_v[b], 1)
                        dve.wait_ge(g_v[b], n * 6 - 1)
                        v.tensor_tensor(gbuf[:, :], gbuf[:, :], E, ALU.mult).then_inc(g_v[b], 1)
                        dve.wait_ge(g_v[b], n * 6)
                        dve.wait_ge(g_C[b], n)
                        v.tensor_tensor(gbuf[:, :], gbuf[:, :], ps[b][1][:, 0:LR], ALU.mult).then_inc(g_m[b], 1)
                        dve.wait_ge(g_m[b], n)
                        v.tensor_tensor(y, y, gbuf[:, :], ALU.add).then_inc(g_y[b], 1)
                        dve.wait_ge(g_y[b], n + 1)

            def tail(b):
                E = xn[b][:, 0:NS * TL]
                w = xn[b][:, NS * TL:2 * NS * TL]
                w3 = w.rearrange("p (n t) -> p n t", t=TL)
                bt = ps[b][0][:, :].rearrange("p (t c n) -> p c n t", c=2, n=NS)
                dve.wait_ge(s_tl, b + 1)
                step(v.tensor_tensor(w3, bt[:, 0], bc(slot(b, K2)[:, LR:L].unsqueeze(1), [128, NS, TL]), ALU.mult))
                dve.wait_ge(s_ET, b + 1)
                step(v.tensor_tensor(w, w, E, ALU.mult))
                v.tensor_scalar(E, E, E_EPS, None, ALU.add)
                step(v.tensor_tensor(w3[:, :, 0], w3[:, :, 0], carry[:, b, :], ALU.add))
                v.reciprocal(E, E)
                dve.wait_ge(s_setx, 2)
                step(v.tensor_tensor_scan(w, seg[:, :, :].rearrange("p n t -> p (n t)"), w, 0.0, ALU.mult, ALU.add))
                step(v.tensor_tensor(w, w, E, ALU.mult))
                step(v.tensor_tensor(w3, w3, bt[:, 1], ALU.mult))
                step(v.reduce_sum(ytail[:, b, :], w3.rearrange("p n t -> p t n"), AX.X))

            def gated(b):
                y = slot(b, K0)
                v.scalar_tensor_tensor(y[:, 0:LR], u[b][:, 0:LR], dpar[:, 0:1], y[:, 0:LR], ALU.mult, ALU.add)
                step(v.scalar_tensor_tensor(y[:, LR:L], u[b][:, LR:L], dpar[:, 0:1], ytail[:, b, :], ALU.mult, ALU.add))
                v.tensor_tensor(slot(b, K1), y, gate[b][:, :], ALU.mult).then_inc(s_yg, 1)

            def norm2(b):
                dve.wait_ge(s_rstd2, b + 1)
                v.tensor_tensor(slot(b, K2)[64:128, :], ps[b][1][64:128, :], slot(b, K1)[64:128, :], ALU.mult
                                ).then_inc(s_xn2, 1)

            constants()
            token_weights()
            tokens(0)
            small_weights()
            norm(0)
            tokens(1)
            swish_conv(0)
            swish_res(0)
            norm(1)
            steps_sum(0)
            swish_conv(1)
            swish_res(1)
            first_state(0)
            general(0)
            tail(0)
            gated(0)
            steps_sum(1)
            norm2(0)
            first_state(1)
            general(1)
            tail(1)
            gated(1)
            norm2(1)


_INS = ["x", "L0_tok_W", "L0_attn_W_in", "L0_attn_conv_k", "L0_attn_conv_b", "L0_attn_W_x", "L0_attn_W_dt",
        "L0_attn_b_dt", "L0_attn_A_log", "L0_attn_D_param", "L0_attn_W_out", "L0_ffn_route_id", "L0_ffn_Wi",
        "L0_ffn_bi", "L0_ffn_Wr", "L0_ffn_br", "L0_ffn_Ws", "L0_ffn_bs", "L0_ffn_Wo", "L0_ffn_bo"]


def shape_constants():
    import numpy as np

    c = np.zeros((128, C_ALL), np.float32)
    eye, mean = np.eye(DM), np.full((DM, DM), 1.0 / DM)
    c[:, C_ID:C_ID + 128] = np.eye(128)
    c[:, C_CC:C_CC + 128] = np.tile(eye - mean, (2, 2))
    c[:, C_IC:C_IC + 128] = np.tile(np.hstack([eye, eye - mean]), (2, 1))
    angle = 2 * np.pi * np.outer(np.arange(NF), np.arange(PATCH)) / PATCH
    c[0:NF, C_DFT:C_DFT + PATCH] = np.cos(angle) / np.sqrt(PATCH)
    c[NF:RIF, C_DFT:C_DFT + PATCH] = -np.sin(angle) / np.sqrt(PATCH)
    c[:, C_IOTA] = np.arange(128)
    return c


def kernel(**inputs):
    import numpy as np
    import concourse.bacc as bacc
    from concourse.bass_utils import run_bass_kernel_spmd

    nc = bacc.Bacc("TRN2", target_bir_lowering=False, num_devices=1)
    arrays, args = {}, []
    for name in _INS:
        a = np.ascontiguousarray(inputs[name])
        arrays[f"in_{name}"] = a
        args.append(nc.dram_tensor(f"in_{name}", a.shape, mybir.dt.from_np(a.dtype), kind="ExternalInput").ap())
    c = shape_constants()
    arrays["shape_constants"] = c
    args.append(nc.dram_tensor("shape_constants", c.shape, mybir.dt.float32, kind="ExternalInput").ap())
    args.append(nc.dram_tensor("out_tokens", (B, L, DM), mybir.dt.float32, kind="ExternalOutput").ap())
    tower(nc, *args)
    r = run_bass_kernel_spmd(nc, [arrays], core_ids=[0])
    return r.results[0]["out_tokens"]
```

```python
import concourse.bass as bass
from concourse import mybir
from contextlib import ExitStack


B, CH, T, V = 2, 64, 128, 64
PATCH, STRIDE = 16, 8
NP = T // STRIDE
L = V * NP
DM = 64
DI = 128
NS = 64
RK = 16
KC = 4
HID, NE, NL = 128, 16, 2
NG = 64
GT = B * L // NG
GB = NG // B
NF = PATCH // 2 + 1
RIF = 2 * NF
TL = 8
LR = L - TL
LN_EPS = 1e-5
E_EPS = 1e-12
ZERO_EXP = -110.0

C_ID, C_CC, C_IC, C_BD, C_DFT, C_IOTA = 0, 128, 192, 320, 448, 464
C_ALL = 465


def tower(nc, x, tok_w, w_in, conv_k, conv_b, w_x, w_dt, b_dt, a_log, d_par, w_out,
          route, wi, bi, wr, br, ws, bs, wo, bo, const, out):
    F32, I32 = mybir.dt.float32, mybir.dt.int32
    ALU, ACT, AX = mybir.AluOpType, mybir.ActivationFunctionType, mybir.AxisListType

    ctx = ExitStack()
    with ctx:
        def sb(name, shape, dt=F32):
            return ctx.enter_context(nc.sbuf_tensor(name, shape, dt))

        def bc(ap, shape):
            return ap.broadcast_to(shape)

        def sem(name):
            return ctx.enter_context(nc.semaphore(name))

        cst = sb("cst", [128, C_ALL])
        xs = sb("xs", [128, B, NP, 4 * V])
        xlast = sb("xlast", [128, B, V])
        early = sb("early", [128, DM * CH])
        wt = early[0:RIF, :].rearrange("p (o c) -> p o c", c=CH)
        weff = sb("weff", [128, 4, 2, DM])
        w_in2 = sb("w_in2", [128, 2 * DI])
        taps = sb("taps", [128, 2, DI])
        w_conv = sb("w_conv", [128, 2, DI])
        cb = sb("cb", [128, 1])
        wx = sb("wx", [DI, RK + 2 * NS])
        wxT = sb("wxT", [RK, DI])
        wdt = sb("wdt", [RK, DI])
        wdelta = sb("wdelta", [DI, DI])
        bdt = sb("bdt", [128, 1])
        nbdt = sb("nbdt", [128, 1])
        alog = sb("alog", [128, NS])
        A = sb("A", [128, NS])
        amax = sb("amax", [128, 1])
        dpar = sb("dpar", [128, 1])
        wout = sb("wout", [DI, 2, DM])
        wmean = sb("wmean", [DI, 1])
        rid = sb("rid", [1, NG], I32)
        ridb = sb("ridb", [NE, NG], I32)
        onehot = sb("onehot", [NE, NG])
        onehott = sb("onehott", [NE + 1, NG, GT])
        wi2 = sb("wi2", [HID, 2, DM])
        wiT = sb("wiT", [128, HID])
        bib = sb("bib", [HID, 1])
        brs = sb("brs", [NE + 1, NL, HID])
        wsh = sb("wsh", [HID, NL, HID])
        wrn = sb("wrn", [HID, NL, NE, HID])
        wexp = sb("wexp", [HID, NE, NL, HID])
        wsel = sb("wsel", [HID, NG, NL, HID])
        won = sb("won", [DM, HID])
        woT = sb("woT", [HID, DM])
        resid = sb("resid", [DM + 1, DM])
        onecol = sb("onecol", [128, 1])
        ceps = sb("ceps", [128, 2])
        rden = [early[:, (1 + b) * L:(1 + b) * L + LR] for b in range(B)]
        rtail = [early[:, 3 * L + b * NS * TL:3 * L + (b + 1) * NS * TL] for b in range(B)]
        warm = sb("warm", [128, 512], mybir.dt.bfloat16)
        gbuf = early[:, 0:LR]
        seg = sb("seg", [128, NS, TL])
        tok = [sb(f"tok{b}", [128, L + 1]) for b in range(B)]
        xn = [sb(f"xn{b}", [128, L + 2]) for b in range(B)]
        u = [sb(f"u{b}", [128, L]) for b in range(B)]
        gate = [wrn[:, 0, 8 * b:8 * b + 8, :].rearrange("p e d -> p (e d)") for b in range(B)]
        h2 = [sb(f"h2{b}", [DM + 1, L]) for b in range(B)]
        carry = sb("carry", [128, B, NS])
        ytail = sb("ytail", [128, B, TL])
        safe = sb("safe", [128, B])
        count = sb("count", [1, B], I32)
        wcur = sb("wcur", [128, 2])
        acur = sb("acur", [128, 1])
        scr = xs[:, :, :, :].rearrange("p b (k s) c -> p b k (s c)", k=4)

        def slot(b, k):
            return scr[:, b, k, :]

        ps = [[ctx.enter_context(nc.psum_tensor(f"ps{b}{p}", [128, L], F32)) for p in range(2)]
              for b in range(B)]

        def weff_to(h, odd):
            return weff[64 * h:64 * h + 64, :, :, :].rearrange("p q a (j e) -> p e a q j", e=2)[:, odd]

        def weff_from(h, odd):
            return ps[0][0][64 * odd:64 * odd + 64, 0:512].rearrange("p (j a h q) -> p h a q j", a=2, h=2, q=4)[:, h]

        names_load = ["s_const", "s_tokw", "s_attw", "s_convw", "s_ffnw", "s_route", "s_x00", "s_x01",
                      "s_x10", "s_x11", "s_ws", "s_wr0", "s_wr1", "s_wr2", "s_wr3"]
        ld = {n: sem(n) for n in names_load}
        s_weff_mm, s_weff = sem("s_weff_mm"), sem("s_weff")
        s_set, s_setx = sem("s_set"), sem("s_setx")
        s_wtr, s_wtrc = sem("s_wtr"), sem("s_wtrc")
        s_wd, s_wdc = sem("s_wd"), sem("s_wdc")
        s_prep = sem("s_prep")
        s_A, s_warm = sem("s_A"), sem("s_warm")
        s_tok, s_tokA, s_tokB = sem("s_tok"), sem("s_tokA"), sem("s_tokB")
        s_cc, s_sq, s_var, s_ln, s_rstd, s_xn = (sem(n) for n in
                                                 ["s_cc", "s_sq", "s_var", "s_ln", "s_rstd", "s_xn"])
        s_xc, s_res, s_u, s_gate = (sem(n) for n in ["s_xc", "s_res", "s_u", "s_gate"])
        s_dz, s_spl, s_dl, s_R = (sem(n) for n in ["s_dz", "s_spl", "s_dl", "s_R"])
        s_safe, s_cnt, s_flag = sem("s_safe"), sem("s_cnt"), sem("s_flag")
        s_B0, s_C0, s_tl = sem("s_B0"), sem("s_C0"), sem("s_tl")
        s_w, s_E, s_rE, s_y0, s_argT, s_ET, s_rET, s_yg = (sem(n) for n in
            ["s_w", "s_E", "s_rE", "s_y0", "s_argT", "s_ET", "s_rET", "s_yg"])
        s_z2, s_h2, s_sq2, s_var2, s_ln2, s_rstd2, s_xn2 = (sem(n) for n in
            ["s_z2", "s_h2", "s_sq2", "s_var2", "s_ln2", "s_rstd2", "s_xn2"])
        s_wi, s_h1, s_l1, s_r1, s_l2, s_r2, s_fin, s_oc, s_out = (sem(n) for n in
            ["s_wi", "s_h1", "s_l1", "s_r1", "s_l2", "s_r2", "s_fin", "s_oc", "s_out"])
        s_t1, s_t1c, s_t2, s_t2c = (sem(n) for n in ["s_t1", "s_t1c", "s_t2", "s_t2c"])
        s_wadd, s_ex, s_exc4 = sem("s_wadd"), sem("s_ex"), sem("s_exc4")
        s_sel = [sem(f"s_sel{b}") for b in range(B)]
        g_cp = [sem(f"g_cp{b}") for b in range(B)]
        g_E = [sem(f"g_E{b}") for b in range(B)]
        g_B = [sem(f"g_B{b}") for b in range(B)]
        g_w = [sem(f"g_w{b}") for b in range(B)]
        g_C = [sem(f"g_C{b}") for b in range(B)]
        g_L = [sem(f"g_L{b}") for b in range(B)]
        g_r = [sem(f"g_r{b}") for b in range(B)]
        g_v = [sem(f"g_v{b}") for b in range(B)]
        g_m = [sem(f"g_m{b}") for b in range(B)]
        g_y = [sem(f"g_y{b}") for b in range(B)]
        s_v, s_a, s_p = sem("s_v"), sem("s_a"), sem("s_p")

        ident = cst[:, C_ID:C_ID + 128]
        c_cc = cst[:, C_CC:C_CC + DM]
        c_bd = cst[:, C_BD:C_BD + 128]
        c_ic = cst[:, C_IC:C_IC + 128]

        x_v = x.rearrange("b c (s h r) v -> b h c s (r v)", h=2, r=4)

        K0, K1, K2, K3 = range(4)

        block = ctx.enter_context(nc.Block())

        @block.sync
        def _(sp):
            sp.dma_start(wt, tok_w.rearrange("o (r c) -> r o c", r=RIF)).then_inc(ld["s_tokw"], 16)
            for b in range(B):
                for k in range(2):
                    sp.dma_start(xs[0:CH, b, 8 * k:8 * k + 8, :], x_v[b, 0, :, 8 * k:8 * k + 8, :]
                                 ).then_inc(ld[f"s_x{b}{k}"], 16)
                sp.dma_start(xlast[0:CH, b, :], x[b, :, T - 1, :]).then_inc(ld[f"s_x{b}1"], 16)
                if b == 0:
                    sp.dma_start(wsh[:, :, :], ws.rearrange("l s h d -> h (l s) d")).then_inc(ld["s_ws"], 16)
            for k in range(4):
                l, e = k // 2, NE // 2 * (k % 2)
                sp.dma_start(wrn[:, l, e:e + NE // 2, :], wr[l, e:e + NE // 2, :, :].rearrange("e h d -> h e d")
                             ).then_inc(ld[f"s_wr{k}"], 16)
            sp.wait_ge(s_exc4, 4)
            sp.wait_ge(ld["s_route"], 32)
            with sp.Fori(0, GB // 4) as i:
                picked = [sp.value_load(rid[0:1, bass.ds(i * 4 + k, 1)], min_val=0, max_val=NE - 1) for k in range(4)]
                for k in range(4):
                    sp.dma_start(wsel[:, bass.ds(i * 4 + k, 1), :, :], wexp[:, bass.ds(picked[k], 1), :, :]
                                 ).then_inc(s_sel[0], 16)
            for b in range(B):
                sp.wait_ge(s_oc, b + 1)
                sp.dma_start(out[b, :, :].rearrange("(p j) o -> p (j o)", j=8), slot(b, K0)[:, 0:8 * DM]
                             ).then_inc(s_out, 16)
            sp.wait_ge(s_out, 16 * B)

        @block.gpsimd
        def _(pool):
            def load(name, to, src):
                pool.dma_start(to, src).then_inc(ld[name], 16)
            load("s_attw", wx[:, :], w_x)
            load("s_attw", wdt[:, :], w_dt)
            load("s_attw", bdt[:, :], b_dt.rearrange("(p a) -> p a", a=1))
            load("s_attw", alog[:, :], a_log)
            load("s_attw", dpar[:, :], d_par.rearrange("(p a) -> p a", a=1))
            load("s_attw", wout[:, 0, :], w_out)
            load("s_ffnw", wi2[:, 0, :], wi)
            load("s_ffnw", wi2[:, 1, :], wi)
            load("s_ffnw", bib[:, :], bi.rearrange("(p a) -> p a", a=1))
            load("s_ffnw", brs[0:NE, :, :], br.rearrange("l e h -> e l h"))
            load("s_ffnw", brs[NE:NE + 1, :, :], bs.rearrange("l s h -> s l h"))
            load("s_ffnw", won[:, :], wo)
            load("s_ffnw", resid[DM:DM + 1, :], bo.rearrange("(a n) -> a n", a=1))
            load("s_route", rid[:, :], route.rearrange("(a n) -> a n", a=1))
            load("s_route", ridb[:, :], route.rearrange("(a n) -> a n", a=1).broadcast_to([NE, NG]))
            pool.memset(seg[:, :, :], 1.0).then_inc(s_p, 1)
            pool.wait_ge(s_p, 1)
            pool.memset(seg[:, :, 0:1], 0.0).then_inc(s_setx, 1)
            pool.memset(carry[:, :, :], 0.0).then_inc(s_setx, 1)
            pool.wait_ge(ld["s_ws"], 16)
            pool.wait_ge(ld["s_const"], 16)
            pool.tensor_tensor(wsh[:, :, :], wsh[:, :, :], bc(ident.unsqueeze(1), [HID, NL, HID]), ALU.add
                               ).then_inc(s_p, 1)
            pool.wait_ge(s_p, 2)
            for k in range(4):
                l, e = k // 2, NE // 2 * (k % 2)
                w = wrn[:, l, e:e + NE // 2, :]
                pool.wait_ge(ld[f"s_wr{k}"], 16)
                pool.tensor_tensor(w, w, bc(wsh[:, l:l + 1, :], [HID, NE // 2, HID]), ALU.add).then_inc(s_wadd, 1)
            pool.wait_ge(s_exc4, 4)
            pool.wait_ge(ld["s_route"], 32)
            with pool.Fori(GB // 4, NG // 4) as i:
                picked = [pool.value_load(rid[0:1, bass.ds(i * 4 + k, 1)], min_val=0, max_val=NE - 1) for k in range(4)]
                for k in range(4):
                    pool.tensor_copy(wsel[:, bass.ds(i * 4 + k, 1), :, :], wexp[:, bass.ds(picked[k], 1), :, :]
                                     ).then_inc(s_sel[1], 1)

        @block.scalar
        def _(act):
            for to, src, name in (
                    [(cst[:, :], const, "s_const")]
                    + [(xs[CH:128, 0, 8 * k:8 * k + 8, :], x_v[0, 1, :, 8 * k:8 * k + 8, :], f"s_x0{k}") for k in range(2)]
                    + [(xlast[CH:128, 0, :], x[0, :, T - 1, :], "s_x01")]
                    + [(w_in2[64 * k:64 * k + 64, :], w_in, "s_convw") for k in range(2)]
                    + [(taps[64 * h:64 * h + 64, k, :], conv_k[3 - 2 * k - h:4 - 2 * k - h, :].broadcast_to([64, DI]), "s_convw")
                       for h in range(2) for k in range(2)]
                    + [(cb[:, :], conv_b.rearrange("(p a) -> p a", a=1), "s_convw")]
                    + [(xs[CH:128, 1, 8 * k:8 * k + 8, :], x_v[1, 1, :, 8 * k:8 * k + 8, :], f"s_x1{k}") for k in range(2)]
                    + [(xlast[CH:128, 1, :], x[1, :, T - 1, :], "s_x11")]):
                act.dma_start(to, src).then_inc(ld[name], 16)
            steps = [0]

            def step(ins):
                ins.then_inc(s_a, 1)
                steps[0] += 1
                act.wait_ge(s_a, steps[0])

            def weights():
                act.wait_ge(s_weff_mm, 1)
                for h in range(2):
                    act.activation(weff_to(h, 0), weff_from(h, 0), ACT.Copy).then_inc(s_weff, 1)
                act.wait_ge(ld["s_attw"], 96)
                step(act.activation(A[:, :], alog[:, :], ACT.Exp))
                act.activation(A[:, :], A[:, :], ACT.Copy, scale=-1.0).then_inc(s_A, 1)

            def tokens(b):
                act.wait_ge(s_tok, b + 1)
                act.activation(tok[b][0:64, 1:].rearrange("p (v n) -> p n v", n=NP),
                               ps[b][0][0:64, :].rearrange("p (n v) -> p n v", v=V), ACT.Copy).then_inc(s_tokA, 1)

            def square(b):
                act.wait_ge(s_cc, b + 1)
                act.activation(slot(b, K0), ps[b][1][:, :], ACT.Square).then_inc(s_sq, 1)

            def rstd(b):
                act.wait_ge(s_var, b + 1)
                act.activation(slot(b, K1), ps[b][0][:, :], ACT.Ln, bias=ceps[:, 0:1]).then_inc(s_ln, 1)
                act.wait_ge(s_ln, b + 1)
                act.activation(slot(b, K1), slot(b, K1), ACT.Exp, scale=-0.5).then_inc(s_rstd, 1)

            def swish(b):
                act.preload_act_table_set("silu_and_others")
                act.wait_ge(s_xc, b + 1)
                act.activation(u[b][:, :], ps[b][1][:, :], ACT.Silu, bias=cb[:, 0:1]).then_inc(s_u, 1)
                act.wait_ge(s_res, b + 1)
                act.activation(gate[b], ps[b][0][:, :], ACT.Silu).then_inc(s_gate, 1)
                act.preload_act_table_set("natural_log_exp_and_others")

            def softplus(b):
                act.wait_ge(s_dz, b + 1)
                step(act.activation(slot(b, K1), ps[b][1][:, :], ACT.Abs, bias=bdt[:, 0:1]))
                step(act.activation(slot(b, K1), slot(b, K1), ACT.Exp, scale=-1.0))
                act.activation(slot(b, K1), slot(b, K1), ACT.Ln, bias=1.0).then_inc(s_spl, 1)

            def decay(b):
                act.wait_ge(s_R, b + 1)
                act.activation(slot(b, K1)[:, 0:LR], slot(b, K3)[:, 0:LR], ACT.Exp, scale=A[:, 0:1]).then_inc(s_E, 1)
                act.wait_ge(s_E, b + 1)
                step(act.activation(rden[b], slot(b, K1)[:, 0:LR], ACT.Ln, bias=ceps[:, 1:2]))
                act.activation(rden[b], rden[b], ACT.Exp, scale=-1.0).then_inc(s_rE, 1)

            def tail_decay(b):
                e, r = xn[b][:, 0:NS * TL], rtail[b]
                act.wait_ge(s_argT, b + 1)
                act.activation(e, e, ACT.Exp).then_inc(s_ET, 1)
                act.wait_ge(s_ET, b + 1)
                step(act.activation(r, e, ACT.Ln, bias=ceps[:, 1:2]))
                act.activation(r, r, ACT.Exp, scale=-1.0).then_inc(s_rET, 1)

            def general(b):
                act.wait_ge(s_flag, b + 1)
                act.wait_ge(s_y0, b + 1)
                lanes = act.value_load(count[0:1, b:b + 1], min_val=0, max_val=128)
                with act.If(lanes < 128):
                    with act.Fori(1, NS) as n:
                        act.wait_ge(g_y[b], n)
                        act.activation(wcur[:, 0:1], wx[:, bass.ds(n + RK, 1)], ACT.Copy).then_inc(g_cp[b], 1)
                        act.activation(wcur[:, 1:2], wx[:, bass.ds(n + RK + NS, 1)], ACT.Copy).then_inc(g_cp[b], 1)
                        act.activation(acur[:, 0:1], A[:, bass.ds(n, 1)], ACT.Copy).then_inc(g_cp[b], 1)
                        act.wait_ge(g_cp[b], n * 3)
                        act.activation(slot(b, K1)[:, 0:LR], slot(b, K3)[:, 0:LR], ACT.Exp, scale=acur[:, 0:1]
                                       ).then_inc(g_E[b], 1)
                        act.wait_ge(g_E[b], n)
                        act.activation(rden[b], slot(b, K1)[:, 0:LR], ACT.Ln, bias=ceps[:, 1:2]
                                       ).then_inc(g_L[b], 1)
                        act.wait_ge(g_L[b], n)
                        act.activation(rden[b], rden[b], ACT.Exp, scale=-1.0).then_inc(g_r[b], 1)

            def norm2(b):
                act.wait_ge(s_z2, b + 1)
                act.activation(slot(b, K0)[64:128, :], ps[b][1][64:128, :], ACT.Square).then_inc(s_sq2, 1)
                act.activation(h2[b][0:DM, :], ps[b][1][0:DM, :], ACT.Copy).then_inc(s_h2, 1)
                act.wait_ge(s_var2, b + 1)
                act.activation(slot(b, K1)[64:128, :], ps[b][0][64:128, :], ACT.Ln, bias=ceps[64:128, 0:1]
                               ).then_inc(s_ln2, 1)
                act.wait_ge(s_ln2, b + 1)
                act.activation(slot(b, K1)[64:128, :], slot(b, K1)[64:128, :], ACT.Exp, scale=-0.5
                               ).then_inc(s_rstd2, 1)

            def relu_in(b):
                act.wait_ge(s_wi, b + 1)
                act.activation(slot(b, K0), ps[b][1][:, :], ACT.Relu, bias=bib[:, 0:1]).then_inc(s_h1, 1)

            def relu_1(b):
                act.wait_ge(s_l1, b + 1)
                act.activation(slot(b, K1), ps[b][0][:, :], ACT.Relu).then_inc(s_r1, 1)

            def relu_2(b):
                act.wait_ge(s_l2, b + 1)
                act.activation(slot(b, K1), ps[b][0][:, :], ACT.Relu).then_inc(s_r2, 1)

            def out_copy(b):
                act.wait_ge(s_fin, b + 1)
                act.activation(slot(b, K0)[:, 0:8 * DM], ps[b][0][:, 0:8 * DM], ACT.Copy).then_inc(s_oc, 1)

            def experts(k):
                l, e = k // 2, NE // 2 * (k % 2)
                act.wait_ge(s_ex, k + 1)
                act.activation(wexp[:, e:e + NE // 2, l, :], ps[1][1 - k % 2][:, :].rearrange("p (e h) -> p e h", h=HID),
                               ACT.Copy).then_inc(s_exc4, 1)

            act.preload_act_table_set("natural_log_exp_and_others")
            weights()
            tokens(0)
            square(0)
            tokens(1)
            act.wait_ge(s_set, 1)
            rstd(0)
            experts(0)
            experts(1)
            experts(2)
            experts(3)
            act.wait_ge(ld["s_convw"], 112)
            swish(0)
            square(1)
            softplus(0)
            rstd(1)
            decay(0)
            tail_decay(0)
            swish(1)
            general(0)
            softplus(1)
            decay(1)
            tail_decay(1)
            norm2(0)
            act.wait_ge(ld["s_ffnw"], 112)
            relu_in(0)
            relu_1(0)
            general(1)
            relu_2(0)
            norm2(1)
            out_copy(0)
            relu_in(1)
            relu_1(1)
            relu_2(1)
            out_copy(1)

        @block.tensor
        def _(pe):
            mm = nc.tensor.matmul

            def halves(pair, lhsT, rhs, n=L, start=True, stop=True):
                for c in range(0, n, 512):
                    last = mm(pair[:, c:min(c + 512, n)], lhsT, rhs[:, c:min(c + 512, n)], start=start, stop=stop)
                return last

            def token_weights():
                pe.wait_ge(ld["s_tokw"], 16)
                pe.wait_ge(ld["s_const"], 16)
                for j in range(DM // 2):
                    last = mm(ps[0][0][:, 16 * j:16 * j + 16], wt[:, 2 * j:2 * j + 2, :],
                              cst[0:RIF, C_DFT:C_DFT + PATCH], start=True, stop=True)
                last.then_inc(s_weff_mm, 1)

            def tokens(b):
                if b == 0:
                    pe.wait_ge(s_weff, 4)
                for k in range(2):
                    pe.wait_ge(ld[f"s_x{b}{k}"], 32 + 32 * k)
                    for q in range(4):
                        mm(ps[b][0][:, 512 * k:512 * k + 512], weff[:, q, :, :],
                           xs[:, b, 8 * k:8 * k + 8, V * q:V * q + V], start=q == 0, stop=q == 3)
                if b == 1:
                    pe.wait_ge(s_prep, 1)
                for q in range(4):
                    last = mm(ps[b][1][:, 0:V], weff[:, q, :, :], xlast[:, b, :], start=q == 0, stop=q == 3)
                last.then_inc(s_tok, 1)

            def small_weights():
                pe.wait_ge(ld["s_attw"], 96)
                nc.tensor.transpose(ps[1][1][0:RK, 0:DI], wx[:, 0:RK], ident)
                pe.wait_ge(ld["s_ffnw"], 112)
                nc.tensor.transpose(ps[1][1][:, 128:128 + HID], wi2[:, :, :], ident)
                nc.tensor.transpose(ps[1][1][:, 256:256 + DM], won[:, :], cst[0:DM, C_ID:C_ID + DM]).then_inc(s_wtr, 1)
                pe.wait_ge(s_wtrc, 1)
                mm(ps[1][1][:, 512:512 + DI], wxT[:, :], wdt[:, :], start=True, stop=True).then_inc(s_wd, 1)

            def centered(b):
                pe.wait_ge(s_tokA, b + 1)
                pe.wait_ge(s_tokB, b + 1)
                for c in range(0, L, 512):
                    for late in range(2):
                        last = mm(ps[b][1][64 * late:64 * late + 64, c:c + 512], c_cc,
                                  tok[b][:, c + 1 - late:c + 513 - late], start=True, stop=True)
                last.then_inc(s_cc, 1)

            def variance(b):
                pe.wait_ge(s_sq, b + 1)
                halves(ps[b][0], c_bd, slot(b, K0)).then_inc(s_var, 1)

            def conv(b):
                pe.wait_ge(s_prep, 1)
                pe.wait_ge(s_xn, b + 1)
                for c in range(0, L, 512):
                    mm(ps[b][1][:, c:c + 512], w_conv[:, 0, :], xn[b][:, c + 2:c + 514], start=True, stop=False)
                    last = mm(ps[b][1][:, c:c + 512], w_conv[:, 1, :], xn[b][:, c:c + 512], start=False, stop=True)
                last.then_inc(s_xc, 1)
                halves(ps[b][0], w_in2[0:64, DI:2 * DI], xn[b][0:64, 2:L + 2]).then_inc(s_res, 1)

            def delta(b):
                pe.wait_ge(s_u, b + 1)
                halves(ps[b][1], wdelta[:, :], u[b]).then_inc(s_dz, 1)

            def first_state(b):
                pe.wait_ge(s_gate, b + 1)
                halves(ps[b][0], bc(wx[:, RK:RK + 1], [DI, 128]), u[b], LR).then_inc(s_B0, 1)
                pe.wait_ge(s_dl, b + 1)
                halves(ps[b][1], bc(wx[:, RK + NS:RK + NS + 1], [DI, 128]), u[b], LR).then_inc(s_C0, 1)

            def safe_lanes(b):
                pe.wait_ge(s_safe, b + 1)
                mm(ps[b][1][0:1, LR + 4:LR + 5], safe[:, b:b + 1], onecol[:, :], start=True, stop=True).then_inc(s_cnt, 1)

            def tail(b):
                pe.wait_ge(s_w, b + 1)
                for t in range(TL):
                    last = mm(ps[b][0][:, 128 * t:128 * t + 128], bc(u[b][:, LR + t:LR + t + 1], [DI, 128]),
                              wx[:, RK:RK + 2 * NS], start=True, stop=True)
                last.then_inc(s_tl, 1)

            def general(b):
                pe.wait_ge(s_flag, b + 1)
                pe.wait_ge(s_y0, b + 1)
                lanes = pe.value_load(count[0:1, b:b + 1], min_val=0, max_val=128)
                with pe.If(lanes < 128):
                    with pe.Fori(1, NS) as n:
                        pe.wait_ge(g_cp[b], n * 3)
                        pe.wait_ge(g_y[b], n)
                        halves(ps[b][1], bc(wcur[:, 0:1], [DI, 128]), u[b], LR).then_inc(g_B[b], 1)
                        pe.wait_ge(g_w[b], n)
                        halves(ps[b][1], bc(wcur[:, 1:2], [DI, 128]), u[b], LR).then_inc(g_C[b], 1)

            def attention_out(b):
                pe.wait_ge(s_yg, b + 1)
                for c in range(0, L, 512):
                    mm(ps[b][1][:, c:c + 512], c_ic, tok[b][:, c + 1:c + 513], start=True, stop=False)
                    last = mm(ps[b][1][:, c:c + 512], wout[:, :, :], slot(b, K1)[:, c:c + 512], start=False, stop=True)
                last.then_inc(s_z2, 1)

            def variance2(b):
                pe.wait_ge(s_sq2, b + 1)
                halves(ps[b][0][64:128, :], c_bd[64:128, 64:128], slot(b, K0)[64:128, :]).then_inc(s_var2, 1)

            def ffn_in(b):
                pe.wait_ge(s_h2, b + 1)
                pe.wait_ge(s_xn2, b + 1)
                halves(ps[b][1], wiT[64:128, :], slot(b, K2)[64:128, :]).then_inc(s_wi, 1)

            def ffn_layer(b, l):
                if l == 0:
                    h = slot(b, K0)
                    pe.wait_ge(s_h1, b + 1)
                    pe.wait_ge(s_sel[b], 16 * GB if b == 0 else GB)
                else:
                    h = slot(b, K2)
                    pe.wait_ge(s_t1c, b + 1)
                per = 128 // GT
                for c in range(L // 128):
                    g0, cols = b * GB + c * per, slice(128 * c, 128 * c + 128)
                    mm(ps[b][0][:, cols], onehott[:, g0:g0 + per, :], brs[:, l, :], start=True, stop=False,
                       skip_group_check=True)
                    for k in range(per):
                        at = 128 * c + GT * k
                        last = mm(ps[b][0][GT * k:GT * k + GT, cols], h[:, at:at + GT], wsel[:, g0 + k, l, :],
                                  start=False, stop=True, skip_group_check=True)
                last.then_inc(s_l1 if l == 0 else s_l2, 1)

            def ffn_turn(b, l):
                pe.wait_ge(s_r1 if l == 0 else s_r2, b + 1)
                for c in range(L // 128):
                    cols = slice(128 * c, 128 * c + 128)
                    last = nc.tensor.transpose(ps[b][1][:, cols], slot(b, K1)[:, cols], ident)
                last.then_inc(s_t1 if l == 0 else s_t2, 1)

            def ffn_out(b):
                pe.wait_ge(s_t2c, b + 1)
                hv = slot(b, K3).rearrange("p (t j) -> p j t", j=8)
                rv = h2[b][:, :].rearrange("p (t j) -> p j t", j=8)
                for j in range(8):
                    mm(ps[b][0][:, DM * j:DM * j + DM], hv[:, j, :], woT[:, :], start=True, stop=False)
                    last = mm(ps[b][0][:, DM * j:DM * j + DM], rv[:, j, :], resid[:, :], start=False, stop=True)
                last.then_inc(s_fin, 1)

            def experts():
                for k in range(4):
                    l, e = k // 2, NE // 2 * (k % 2)
                    pe.wait_ge(s_wadd, k + 1)
                    if k >= 2:
                        pe.wait_ge(s_exc4, k - 1)
                    for i in range(NE // 2):
                        last = nc.tensor.transpose(ps[1][1 - k % 2][:, 128 * i:128 * i + 128], wrn[:, l, e + i, :], ident)
                    last.then_inc(s_ex, 1)

            pe.wait_ge(s_warm, 1)
            for _ in range(16):
                mm(ps[1][0][:, 0:512], warm[:, 0:128], warm[:, :], start=True, stop=True)
            token_weights()
            tokens(0)
            small_weights()
            centered(0)
            tokens(1)
            variance(0)
            pe.wait_ge(s_tokA, 2)
            pe.wait_ge(s_tokB, 2)
            experts()
            conv(0)
            pe.wait_ge(s_exc4, 4)
            centered(1)
            variance(1)
            delta(0)
            first_state(0)
            safe_lanes(0)
            conv(1)
            tail(0)
            general(0)
            delta(1)
            attention_out(0)
            first_state(1)
            safe_lanes(1)
            variance2(0)
            tail(1)
            ffn_in(0)
            ffn_layer(0, 0)
            general(1)
            ffn_turn(0, 0)
            ffn_layer(0, 1)
            attention_out(1)
            ffn_turn(0, 1)
            variance2(1)
            ffn_out(0)
            ffn_in(1)
            ffn_layer(1, 0)
            ffn_turn(1, 0)
            ffn_layer(1, 1)
            ffn_turn(1, 1)
            ffn_out(1)

        @block.vector
        def _(dve):
            v = nc.vector
            steps = [0]

            def step(ins):
                ins.then_inc(s_v, 1)
                steps[0] += 1
                dve.wait_ge(s_v, steps[0])

            def constants():
                v.memset(warm[:, :], 0.0).then_inc(s_warm, 1)
                v.memset(onecol[:, :], 1.0)
                v.memset(ceps[:, 0:1], LN_EPS)
                for b in range(B):
                    v.memset(xn[b][:, 0:2], 0.0)
                    v.memset(tok[b][:, 0:1], 0.0)
                    v.memset(h2[b][DM:DM + 1, :], 1.0)
                v.memset(onehott[:, :, :], 1.0)
                v.memset(ceps[:, 1:2], E_EPS).then_inc(s_set, 1)

            def token_weights():
                dve.wait_ge(s_weff_mm, 1)
                for h in range(2):
                    v.tensor_copy(weff_to(h, 1), weff_from(h, 1)).then_inc(s_weff, 1)

            def small_weights():
                dve.wait_ge(ld["s_convw"], 112)
                v.tensor_tensor(w_conv[:, :, :], bc(w_in2[:, 0:DI].unsqueeze(1), [128, 2, DI]), taps[:, :, :], ALU.mult)
                dve.wait_ge(s_wtr, 1)
                v.tensor_copy(wxT[:, :], ps[1][1][0:RK, 0:DI]).then_inc(s_wtrc, 1)
                v.tensor_copy(wiT[:, :], ps[1][1][:, 128:128 + HID])
                v.tensor_copy(woT[:, :], ps[1][1][:, 256:256 + DM])
                v.tensor_scalar(nbdt[:, :], bdt[:, :], -1.0, None, ALU.mult)
                step(v.reduce_sum(wmean[:, :], wout[:, 0, :], AX.X))
                v.memset(resid[0:DM, :], 0.0)
                step(v.tensor_scalar(wmean[:, :], wmean[:, :], 1.0 / DM, None, ALU.mult))
                v.tensor_scalar(wout[:, 1, :], wout[:, 0, :], wmean[:, 0:1], None, ALU.subtract)
                v.tensor_copy(resid[0:DM, :], cst[0:DM, C_ID:C_ID + DM])
                dve.wait_ge(s_A, 1)
                v.reduce_max(amax[:, :], A[:, 1:NS], AX.X)
                dve.wait_ge(ld["s_route"], 32)
                dve.wait_ge(s_set, 1)
                step(v.tensor_scalar(onehot[:, :], ridb[:, :], cst[0:NE, C_IOTA:C_IOTA + 1], None, ALU.is_equal))
                v.tensor_copy(onehott[0:NE, :, :], bc(onehot[:, :].unsqueeze(2), [NE, NG, GT]))
                dve.wait_ge(s_wd, 1)
                v.tensor_copy(wdelta[:, :], ps[1][1][:, 512:512 + DI]).then_inc(s_prep, 1)

            def tokens(b):
                dve.wait_ge(s_tok, b + 1)
                to = tok[b][64:128, 1:].rearrange("p (v n) -> p n v", n=NP)
                v.tensor_copy(to[:, 0:NP - 1, :], ps[b][0][64:128, V:L].rearrange("p (n v) -> p n v", v=V))
                v.tensor_copy(to[:, NP - 1, :], ps[b][1][64:128, 0:V]).then_inc(s_tokB, 1)

            def norm(b):
                dve.wait_ge(s_rstd, b + 1)
                v.tensor_tensor(xn[b][:, 2:L + 2], ps[b][1][:, :], slot(b, K1), ALU.mult).then_inc(s_xn, 1)

            def steps_sum(b):
                dve.wait_ge(s_spl, b + 1)
                v.scalar_tensor_tensor(slot(b, K0), ps[b][1][:, :], nbdt[:, 0:1], slot(b, K1), ALU.max, ALU.add
                                       ).then_inc(s_dl, 1)
                dve.wait_ge(s_dl, b + 1)
                v.memset(slot(b, K3)[:, L - 1:L], 0.0)
                step(v.tensor_tensor_scan(slot(b, K3)[:, 0:L - 1][:, ::-1], slot(b, K0)[:, 1:L][:, ::-1],
                                          bc(bdt[:, 0:1], [128, L - 1]), 0.0, ALU.add, ALU.add))
                v.scalar_tensor_tensor(slot(b, K2), slot(b, K0), bdt[:, 0:1], u[b][:, :], ALU.add, ALU.mult
                                       ).then_inc(s_R, 1)
                step(v.tensor_scalar(safe[:, b:b + 1], amax[:, 0:1], slot(b, K3)[:, LR - 1:LR], None, ALU.mult))
                v.tensor_scalar(safe[:, b:b + 1], safe[:, b:b + 1], ZERO_EXP, None, ALU.is_le).then_inc(s_safe, 1)
                v.tensor_tensor(xn[b][:, 0:NS * TL].rearrange("p (n t) -> p n t", t=TL),
                                bc(slot(b, K3)[:, LR:L].unsqueeze(1), [128, NS, TL]),
                                bc(A[:, :].unsqueeze(2), [128, NS, TL]), ALU.mult).then_inc(s_argT, 1)

            def first_state(b):
                dve.wait_ge(s_B0, b + 1)
                dve.wait_ge(s_R, b + 1)
                w = slot(b, K0)[:, 0:LR]
                v.tensor_tensor(w, ps[b][0][:, 0:LR], slot(b, K2)[:, 0:LR], ALU.mult).then_inc(s_w, 1)
                dve.wait_ge(s_w, b + 1)
                dve.wait_ge(s_E, b + 1)
                step(v.tensor_tensor(w, w, slot(b, K1)[:, 0:LR], ALU.mult))
                step(v.tensor_tensor_scan(w, bc(onecol[:, 0:1], [128, LR]), w, 0.0, ALU.mult, ALU.add))
                dve.wait_ge(s_setx, 2)
                step(v.tensor_copy(carry[:, b, 0:1], slot(b, K0)[:, LR - 1:LR]))
                dve.wait_ge(s_cnt, b + 1)
                v.tensor_copy(count[0:1, b:b + 1], ps[b][1][0:1, LR + 4:LR + 5]).then_inc(s_flag, 1)
                dve.wait_ge(s_rE, b + 1)
                step(v.tensor_tensor(w, w, rden[b], ALU.mult))
                dve.wait_ge(s_C0, b + 1)
                v.tensor_tensor(w, w, ps[b][1][:, 0:LR], ALU.mult).then_inc(s_y0, 1)
                dve.wait_ge(s_y0, b + 1)

            def general(b):
                dve.wait_ge(s_flag, b + 1)
                lanes = dve.value_load(count[0:1, b:b + 1], min_val=0, max_val=128)
                y, E = slot(b, K0)[:, 0:LR], slot(b, K1)[:, 0:LR]
                with dve.If(lanes < 128):
                    v.memset(gbuf[:, 0:1], 0.0).then_inc(g_y[b], 1)
                    dve.wait_ge(g_y[b], 1)
                    with dve.Fori(1, NS) as n:
                        dve.wait_ge(g_B[b], n)
                        v.tensor_tensor(gbuf, ps[b][1][:, 0:LR], slot(b, K2)[:, 0:LR], ALU.mult
                                        ).then_inc(g_w[b], 1)
                        dve.wait_ge(g_w[b], n)
                        dve.wait_ge(g_E[b], n)
                        v.tensor_tensor(gbuf, gbuf, E, ALU.mult).then_inc(g_v[b], 1)
                        dve.wait_ge(g_v[b], n * 4 - 3)
                        v.tensor_tensor_scan(gbuf, bc(onecol[:, 0:1], [128, LR]), gbuf, 0.0,
                                             ALU.mult, ALU.add).then_inc(g_v[b], 1)
                        dve.wait_ge(g_v[b], n * 4 - 2)
                        v.tensor_copy(carry[:, b, bass.ds(n, 1)], gbuf[:, LR - 1:LR]).then_inc(g_v[b], 1)
                        dve.wait_ge(g_v[b], n * 4 - 1)
                        dve.wait_ge(g_r[b], n)
                        v.tensor_tensor(gbuf, gbuf, rden[b], ALU.mult).then_inc(g_v[b], 1)
                        dve.wait_ge(g_v[b], n * 4)
                        dve.wait_ge(g_C[b], n)
                        v.tensor_tensor(gbuf, gbuf, ps[b][1][:, 0:LR], ALU.mult).then_inc(g_m[b], 1)
                        dve.wait_ge(g_m[b], n)
                        v.tensor_tensor(y, y, gbuf, ALU.add).then_inc(g_y[b], 1)
                        dve.wait_ge(g_y[b], n + 1)

            def tail(b):
                E = xn[b][:, 0:NS * TL]
                w = xn[b][:, NS * TL:2 * NS * TL]
                w3 = w.rearrange("p (n t) -> p n t", t=TL)
                bt = ps[b][0][:, :].rearrange("p (t c n) -> p c n t", c=2, n=NS)
                dve.wait_ge(s_tl, b + 1)
                step(v.tensor_tensor(w3, bt[:, 0], bc(slot(b, K2)[:, LR:L].unsqueeze(1), [128, NS, TL]), ALU.mult))
                dve.wait_ge(s_ET, b + 1)
                step(v.tensor_tensor(w, w, E, ALU.mult))
                step(v.tensor_tensor(w3[:, :, 0], w3[:, :, 0], carry[:, b, :], ALU.add))
                step(v.tensor_tensor_scan(w, seg[:, :, :].rearrange("p n t -> p (n t)"), w, 0.0, ALU.mult, ALU.add))
                dve.wait_ge(s_rET, b + 1)
                step(v.tensor_tensor(w, w, rtail[b], ALU.mult))
                step(v.tensor_tensor(w3, w3, bt[:, 1], ALU.mult))
                step(v.reduce_sum(ytail[:, b, :], w3.rearrange("p n t -> p t n"), AX.X))

            def gated(b):
                y = slot(b, K0)
                v.scalar_tensor_tensor(y[:, 0:LR], u[b][:, 0:LR], dpar[:, 0:1], y[:, 0:LR], ALU.mult, ALU.add)
                step(v.scalar_tensor_tensor(y[:, LR:L], u[b][:, LR:L], dpar[:, 0:1], ytail[:, b, :], ALU.mult, ALU.add))
                v.tensor_tensor(slot(b, K1), y, gate[b], ALU.mult).then_inc(s_yg, 1)

            def ffn_copy(b, l):
                dve.wait_ge(s_t1 if l == 0 else s_t2, b + 1)
                v.tensor_copy(slot(b, K2 if l == 0 else K3), ps[b][1][:, :]).then_inc(s_t1c if l == 0 else s_t2c, 1)

            def norm2(b):
                dve.wait_ge(s_rstd2, b + 1)
                v.tensor_tensor(slot(b, K2)[64:128, :], ps[b][1][64:128, :], slot(b, K1)[64:128, :], ALU.mult
                                ).then_inc(s_xn2, 1)

            constants()
            token_weights()
            tokens(0)
            small_weights()
            tokens(1)
            norm(0)
            norm(1)
            steps_sum(0)
            first_state(0)
            general(0)
            tail(0)
            gated(0)
            steps_sum(1)
            first_state(1)
            norm2(0)
            general(1)
            tail(1)
            gated(1)
            ffn_copy(0, 0)
            norm2(1)
            ffn_copy(0, 1)
            ffn_copy(1, 0)
            ffn_copy(1, 1)


_INS = ["x", "L0_tok_W", "L0_attn_W_in", "L0_attn_conv_k", "L0_attn_conv_b", "L0_attn_W_x", "L0_attn_W_dt",
        "L0_attn_b_dt", "L0_attn_A_log", "L0_attn_D_param", "L0_attn_W_out", "L0_ffn_route_id", "L0_ffn_Wi",
        "L0_ffn_bi", "L0_ffn_Wr", "L0_ffn_br", "L0_ffn_Ws", "L0_ffn_bs", "L0_ffn_Wo", "L0_ffn_bo"]


def shape_constants():
    import numpy as np

    c = np.zeros((128, C_ALL), np.float32)
    eye, mean = np.eye(DM), np.full((DM, DM), 1.0 / DM)
    c[:, C_ID:C_ID + 128] = np.eye(128)
    c[:, C_CC:C_CC + DM] = np.tile(eye - mean, (2, 1))
    c[:, C_BD:C_BD + 128] = np.kron(np.eye(2), mean)
    c[:, C_IC:C_IC + 128] = np.tile(np.hstack([eye, eye - mean]), (2, 1))
    angle = 2 * np.pi * np.outer(np.arange(NF), np.arange(PATCH)) / PATCH
    c[0:NF, C_DFT:C_DFT + PATCH] = np.cos(angle) / np.sqrt(PATCH)
    c[NF:RIF, C_DFT:C_DFT + PATCH] = -np.sin(angle) / np.sqrt(PATCH)
    c[:, C_IOTA] = np.arange(128)
    return c


def kernel(**inputs):
    import numpy as np
    import concourse.bacc as bacc
    from concourse.bass_utils import run_bass_kernel_spmd

    nc = bacc.Bacc("TRN2", target_bir_lowering=False, num_devices=1)
    arrays, args = {}, []
    for name in _INS:
        a = np.ascontiguousarray(inputs[name])
        arrays[f"in_{name}"] = a
        args.append(nc.dram_tensor(f"in_{name}", a.shape, mybir.dt.from_np(a.dtype), kind="ExternalInput").ap())
    c = shape_constants()
    arrays["shape_constants"] = c
    args.append(nc.dram_tensor("shape_constants", c.shape, mybir.dt.float32, kind="ExternalInput").ap())
    args.append(nc.dram_tensor("out_tokens", (B, L, DM), mybir.dt.float32, kind="ExternalOutput").ap())
    tower(nc, *args)
    r = run_bass_kernel_spmd(nc, [arrays], core_ids=[0])
    return r.results[0]["out_tokens"]
```

```python
import concourse.bass as bass
from concourse import mybir
from contextlib import ExitStack


B, CH, T, V = 2, 64, 128, 64
PATCH, STRIDE = 16, 8
NP = T // STRIDE
L = V * NP
DM = 64
DI = 128
NS = 64
RK = 16
KC = 4
HID, NE, NL = 128, 16, 2
NG = 64
GT = B * L // NG
GB = NG // B
NF = PATCH // 2 + 1
RIF = 2 * NF
TL = 8
LR = L - TL
HL = L // 2
LN_EPS = 1e-5
E_EPS = 1e-12
ZERO_EXP = -110.0

C_ID, C_CC, C_IC, C_BD, C_DFT, C_IOTA, C_SHARED = 0, 128, 192, 320, 448, 512, 513
C_ALL = 514


def tower(nc, x, tok_w, w_in, conv_k, conv_b, w_x, w_dt, b_dt, a_log, d_par, w_out,
          route, wi, bi, wr, br, ws, bs, wo, bo, const, out):
    F32, I32, BF16 = mybir.dt.float32, mybir.dt.int32, mybir.dt.bfloat16
    ALU, ACT, AX = mybir.AluOpType, mybir.ActivationFunctionType, mybir.AxisListType

    ctx = ExitStack()
    with ctx:
        def sb(name, shape, dt=F32):
            return ctx.enter_context(nc.sbuf_tensor(name, shape, dt))

        def bc(ap, shape):
            return ap.broadcast_to(shape)

        def sem(name):
            return ctx.enter_context(nc.semaphore(name))

        cst = sb("cst", [128, C_ALL])
        xs = sb("xs", [128, B, NP, 4 * V])
        xlast = sb("xlast", [128, B, V])
        early = sb("early", [128, DM * CH])
        wt = early[0:4 * RIF, 0:DM // 4 * CH]
        weff = sb("weff", [128, 4, 2, DM])
        wlast = sb("wlast", [128, 2 * DM])
        w_in2 = sb("w_in2", [128, 2 * DI])
        taps = sb("taps", [128, 2, DI])
        w_conv = sb("w_conv", [128, 2, DI])
        cb = sb("cb", [128, 1])
        wx = sb("wx", [DI, RK + 2 * NS])
        wxT = sb("wxT", [RK, DI])
        wdt = sb("wdt", [RK, DI])
        wdelta = sb("wdelta", [DI, DI])
        bdt = sb("bdt", [128, 1])
        nbdt = sb("nbdt", [128, 1])
        alog = sb("alog", [128, NS])
        A = sb("A", [128, NS])
        amax = sb("amax", [128, 1])
        dpar = sb("dpar", [128, 1])
        wout = sb("wout", [DI, 2, DM])
        wmean = sb("wmean", [DI, 1])
        rid = sb("rid", [1, NG], I32)
        ridb = sb("ridb", [96, NG], I32)
        onehot = sb("onehot", [96, NG])
        onehott = sb("onehott", [96, NG, GT], BF16)
        brest = sb("brest", [96, NL, HID])
        bparts = sb("bparts", [96, NL, HID], BF16)
        wi2 = sb("wi2", [HID, 2, DM])
        wiT = sb("wiT", [128, HID])
        bib = sb("bib", [HID, 1])
        wsh = sb("wsh", [HID, NL, HID])
        wrn = sb("wrn", [HID, NL, NE, HID])
        wexp = sb("wexp", [HID, NE, NL, HID])
        wsel = sb("wsel", [HID, NG, NL, HID])
        won = sb("won", [DM, HID])
        woT = sb("woT", [HID, DM])
        bob = sb("bob", [DM, 1])
        onecol = sb("onecol", [128, 1])
        ceps = sb("ceps", [128, 2])
        rden = [sb("rden0", [128, LR]), wrn[:, 0, 0:8, :].rearrange("p e d -> p (e d)")[:, 0:LR]]
        rtail = [early[:, 3 * L + b * NS * TL:3 * L + (b + 1) * NS * TL] for b in range(B)]
        tprod = [wrn[:, 1, 8 * b:8 * b + 8, :].rearrange("p e d -> p (e d)") for b in range(B)]
        ones = bc(onecol[:, 0:1], [128, 128])
        warm = sb("warm", [128, 512], BF16)
        gbuf = early[:, 0:LR]
        seg = sb("seg", [128, NS, TL])
        tok = [sb(f"tok{b}", [128, L + 1]) for b in range(B)]
        xn = [sb(f"xn{b}", [128, L + 2]) for b in range(B)]
        u = [sb(f"u{b}", [128, L]) for b in range(B)]
        gate = [early[:, (1 + b) * L:(2 + b) * L] for b in range(B)]
        h2 = [sb(f"h2{b}", [DM, L]) for b in range(B)]
        carry = sb("carry", [128, B, NS])
        ytail = sb("ytail", [128, B, TL])
        safe = sb("safe", [128, B])
        count = sb("count", [1, B], I32)
        wcur = sb("wcur", [128, 2])
        acur = sb("acur", [128, 1])
        scr = xs[:, :, :, :].rearrange("p b (k s) c -> p b k (s c)", k=4)

        def slot(b, k):
            return scr[:, b, k, :]

        ps = [[ctx.enter_context(nc.psum_tensor(f"ps{b}{p}", [128, L], F32)) for p in range(2)]
              for b in range(B)]

        def weff_to(h, odd):
            v = weff[64 * h:64 * h + 64, :, :, :].rearrange("p q a (k j e) -> p e (q a) k j", k=4, e=2)
            return v[:, odd]

        def weff_from(h, odd):
            v = ps[0][0][64 * odd:64 * odd + 64, 0:HL].rearrange("p (j k h r) -> p h r k j", k=4, h=2, r=8)
            return v[:, h]

        def at(b, c):
            return 2 * b + c + 1

        def back(b, c):
            return 2 * b + 2 - c

        def half(ap, c, n=L):
            return ap[:, HL * c:min(HL * c + HL, n)]

        names_load = ["s_const", "s_tokw", "s_attw", "s_convw", "s_wio", "s_bias", "s_ffnw", "s_route", "s_x00", "s_x01",
                      "s_x10", "s_x11", "s_ws", "s_wr0", "s_wr1", "s_wr2", "s_wr3"]
        ld = {n: sem(n) for n in names_load}
        s_weff_mm, s_weff, s_wlast = sem("s_weff_mm"), sem("s_weff"), sem("s_wlast")
        s_set, s_setx = sem("s_set"), sem("s_setx")
        s_wtr, s_wtrc = sem("s_wtr"), sem("s_wtrc")
        s_wd, s_wconv, s_onehot = sem("s_wd"), sem("s_wconv"), sem("s_onehot")
        s_prep = sem("s_prep")
        s_A, s_warm = sem("s_A"), sem("s_warm")
        s_tok, s_tokA, s_tokB = sem("s_tok"), sem("s_tokA"), sem("s_tokB")
        s_cc, s_sq, s_var, s_ln, s_rstd, s_xn = (sem(n) for n in
                                                 ["s_cc", "s_sq", "s_var", "s_ln", "s_rstd", "s_xn"])
        s_xc, s_res, s_u, s_gate = (sem(n) for n in ["s_xc", "s_res", "s_u", "s_gate"])
        s_dz, s_spl, s_dl, s_R, s_du, s_carry, s_wE, s_sum, s_wr, s_tail = (sem(n) for n in
                                                 ["s_dz", "s_spl", "s_dl", "s_R", "s_du", "s_carry", "s_wE", "s_sum", "s_wr", "s_tail"])
        s_safe, s_cnt, s_flag = sem("s_safe"), sem("s_cnt"), sem("s_flag")
        s_B0, s_C0, s_tl = sem("s_B0"), sem("s_C0"), sem("s_tl")
        s_w, s_E, s_lE, s_rE, s_y0, s_argT, s_ET, s_rET, s_ysum, s_yg, s_tprod = (sem(n) for n in
            ["s_w", "s_E", "s_lE", "s_rE", "s_y0", "s_argT", "s_ET", "s_rET", "s_ysum", "s_yg", "s_tprod"])
        s_z2, s_h2, s_sq2, s_var2, s_ln2, s_rstd2, s_xn2 = (sem(n) for n in
            ["s_z2", "s_h2", "s_sq2", "s_var2", "s_ln2", "s_rstd2", "s_xn2"])
        s_wi, s_h1, s_l1, s_r1, s_l2, s_r2, s_resid, s_residc, s_fin, s_oc, s_out = (sem(n) for n in
            ["s_wi", "s_h1", "s_l1", "s_r1", "s_l2", "s_r2", "s_resid", "s_residc", "s_fin", "s_oc", "s_out"])
        s_t1, s_t1c, s_t2, s_t2c = (sem(n) for n in ["s_t1", "s_t1c", "s_t2", "s_t2c"])
        s_ex, s_exc = sem("s_ex"), sem("s_exc")
        s_bparts = sem("s_bparts")
        s_sel0 = sem("s_sel0")
        s_sel1 = [sem(f"s_sel1{b}") for b in range(B)]

        g_cp = [sem(f"g_cp{b}") for b in range(B)]
        g_E = [sem(f"g_E{b}") for b in range(B)]
        g_B = [sem(f"g_B{b}") for b in range(B)]
        g_w = [sem(f"g_w{b}") for b in range(B)]
        g_C = [sem(f"g_C{b}") for b in range(B)]
        g_L = [sem(f"g_L{b}") for b in range(B)]
        g_r = [sem(f"g_r{b}") for b in range(B)]
        g_v = [sem(f"g_v{b}") for b in range(B)]
        g_m = [sem(f"g_m{b}") for b in range(B)]
        g_y = [sem(f"g_y{b}") for b in range(B)]
        s_v, s_a, s_p = sem("s_v"), sem("s_a"), sem("s_p")

        ident = cst[:, C_ID:C_ID + 128]
        c_cc = cst[:, C_CC:C_CC + DM]
        c_bd = cst[:, C_BD:C_BD + 128]
        c_ic = cst[:, C_IC:C_IC + 128]

        x_v = x.rearrange("b c (s h r) v -> b h c s (r v)", h=2, r=4)

        K0, K1, K2, K3 = range(4)

        def load_token_weights(queue, k):
            queue.dma_start(wt[RIF * k:RIF * k + RIF, :].rearrange("p (o c) -> p o c", c=CH),
                            tok_w[16 * k:16 * k + 16, :].rearrange("o (r c) -> r o c", r=RIF)).then_inc(ld["s_tokw"], 16)

        block = ctx.enter_context(nc.Block())

        @block.sync
        def _(sp):
            for k in range(2):
                load_token_weights(sp, k)
            for b in range(B):
                for k in range(2):
                    for h in range(b + 1):
                        sp.dma_start(xs[CH * h:CH * h + CH, b, 8 * k:8 * k + 8, :], x_v[b, h, :, 8 * k:8 * k + 8, :]
                                     ).then_inc(ld[f"s_x{b}{k}"], 16)
                for h in range(b + 1):
                    sp.dma_start(xlast[CH * h:CH * h + CH, b, :], x[b, :, T - 1, :]).then_inc(ld[f"s_x{b}1"], 16)
                if b == 0:
                    sp.dma_start(wsh[:, :, :], ws.rearrange("l s h d -> h (l s) d")).then_inc(ld["s_ws"], 16)
                    for k in range(2):
                        sp.dma_start(wi2[:, k, :], wi).then_inc(ld["s_wio"], 16)
                    sp.dma_start(won[:, :], wo).then_inc(ld["s_wio"], 16)
            for k in range(4):
                l, e = k // 2, NE // 2 * (k % 2)
                sp.dma_start(wrn[:, l, e:e + NE // 2, :], wr[l, e:e + NE // 2, :, :].rearrange("e h d -> h e d")
                             ).then_inc(ld[f"s_wr{k}"], 16)
            sp.wait_ge(s_exc, 8)
            sp.wait_ge(ld["s_route"], 32)
            for b in range(B):
                with sp.Fori((2 * b + 1) * GB // 8, (2 * b + 2) * GB // 8) as i:
                    picked = [sp.value_load(rid[0:1, bass.ds(i * 4 + k, 1)], min_val=0, max_val=NE - 1) for k in range(4)]
                    for k in range(4):
                        sp.dma_start(wsel[:, bass.ds(i * 4 + k, 1), :, :], wexp[:, bass.ds(picked[k], 1), :, :]
                                     ).then_inc(s_sel1[b], 16)
            for b in range(B):
                for c in range(2):
                    sp.wait_ge(s_oc, at(b, c))
                    sp.dma_start(out[b, HL * c:HL * c + HL, :].rearrange("(p j) o -> p (j o)", j=4),
                                 half(slot(b, K0), c)[:, 0:4 * DM]).then_inc(s_out, 16)
            sp.wait_ge(s_out, 32 * B)

        @block.gpsimd
        def _(pool):
            def load(name, to, src):
                pool.dma_start(to, src).then_inc(ld[name], 16)
            load("s_const", cst[:, :], const)
            for h in range(2):
                load("s_convw", w_in2[64 * h:64 * h + 64, :], w_in)
            for h in range(2):
                load("s_convw", taps[64 * h:64 * h + 64, :, :], conv_k.rearrange("(k e) d -> e k d", e=2)[1 - h:2 - h, :, :]
                     .broadcast_to([64, 2, DI]))
            load("s_convw", cb[:, :], conv_b.rearrange("(p a) -> p a", a=1))
            load("s_attw", wx[:, :], w_x)
            load("s_attw", wdt[:, :], w_dt)
            load("s_attw", bdt[:, :], b_dt.rearrange("(p a) -> p a", a=1))
            load("s_attw", alog[:, :], a_log)
            load("s_attw", dpar[:, :], d_par.rearrange("(p a) -> p a", a=1))
            load("s_attw", wout[:, 0, :], w_out)
            load("s_route", rid[:, :], route.rearrange("(a n) -> a n", a=1))
            load("s_route", ridb[:, :], route.rearrange("(a n) -> a n", a=1).broadcast_to([96, NG]))
            load("s_ffnw", bib[:, :], bi.rearrange("(p a) -> p a", a=1))
            load("s_ffnw", bob[:, :], bo.rearrange("(p a) -> p a", a=1))
            pool.wait_ge(s_set, 1)
            for q in (0, 32, 64):
                load("s_bias", brest[q:q + NE, :, :], br.rearrange("l e h -> e l h"))
                load("s_bias", brest[q + NE:q + NE + 1, :, :], bs.rearrange("l s h -> s l h"))
            pool.memset(seg[:, :, :], 1.0).then_inc(s_p, 1)
            pool.wait_ge(s_p, 1)
            pool.memset(seg[:, :, 0:1], 0.0).then_inc(s_setx, 1)
            pool.memset(carry[:, :, :], 0.0).then_inc(s_setx, 1)
            steps = [1]

            def step(ins):
                ins.then_inc(s_p, 1)
                steps[0] += 1
                pool.wait_ge(s_p, steps[0])
            pool.wait_ge(ld["s_bias"], 96)
            step(pool.tensor_copy(bparts[:, :, :], brest[:, :, :]))
            for q in (32, 64):
                step(pool.tensor_tensor(brest[q:q + 32], brest[q:q + 32], bparts[q:q + 32], ALU.subtract))
                step(pool.tensor_copy(bparts[q:q + 32], brest[q:q + 32]))
            step(pool.tensor_tensor(brest[64:96], brest[64:96], bparts[64:96], ALU.subtract))
            pool.tensor_copy(bparts[64:96], brest[64:96]).then_inc(s_bparts, 1)
            pool.wait_ge(s_bparts, 1)
            pool.wait_ge(s_exc, 8)
            pool.wait_ge(ld["s_route"], 32)
            for b in range(B):
                pool.wait_ge(s_u, 2 * b + 2)
                pool.tensor_tensor(tprod[b].rearrange("p (t n) -> p t n", t=TL),
                                   bc(wx[:, RK:RK + 2 * NS].unsqueeze(1), [DI, TL, 2 * NS]),
                                   bc(u[b][:, LR:L].unsqueeze(2), [DI, TL, 2 * NS]), ALU.mult).then_inc(s_tprod, 1)
                pool.wait_ge(s_A, 1)
                pool.wait_ge(s_R, 2 * b + 1)
                pool.tensor_tensor(xn[b][:, 0:NS * TL].rearrange("p (n t) -> p n t", t=TL),
                                   bc(slot(b, K3)[:, LR:L].unsqueeze(1), [128, NS, TL]),
                                   bc(A[:, :].unsqueeze(2), [128, NS, TL]), ALU.mult).then_inc(s_argT, 1)
                with pool.Fori(2 * b * GB // 8, (2 * b + 1) * GB // 8) as i:
                    picked = [pool.value_load(rid[0:1, bass.ds(i * 4 + k, 1)], min_val=0, max_val=NE - 1) for k in range(4)]
                    for k in range(4):
                        pool.tensor_copy(wsel[:, bass.ds(i * 4 + k, 1), :, :], wexp[:, bass.ds(picked[k], 1), :, :]
                                         ).then_inc(s_sel0, 1)

        @block.scalar
        def _(act):
            for k in range(2, 4):
                load_token_weights(act, k)
            for k in range(2):
                act.dma_start(xs[CH:128, 0, 8 * k:8 * k + 8, :], x_v[0, 1, :, 8 * k:8 * k + 8, :]).then_inc(ld[f"s_x0{k}"], 16)
            act.dma_start(xlast[CH:128, 0, :], x[0, :, T - 1, :]).then_inc(ld["s_x01"], 16)
            steps = [0]

            def step(ins):
                ins.then_inc(s_a, 1)
                steps[0] += 1
                act.wait_ge(s_a, steps[0])

            def weights():
                act.wait_ge(s_weff_mm, 1)
                for h in range(2):
                    act.activation(weff_to(h, 0), weff_from(h, 0), ACT.Copy).then_inc(s_weff, 1)

            def decay_rates():
                act.wait_ge(ld["s_attw"], 96)
                step(act.activation(A[:, :], alog[:, :], ACT.Exp))
                act.activation(A[:, :], A[:, :], ACT.Copy, scale=-1.0).then_inc(s_A, 1)

            def tokens(b, c):
                to = tok[b][0:64, 1:].rearrange("p (v n) -> p n v", n=NP)
                act.wait_ge(s_tok, 3 * b + c + 1)
                act.activation(to[:, 8 * c:8 * c + 8, :], half(ps[b][0], c)[0:64, :].rearrange("p (n v) -> p n v", v=V),
                               ACT.Copy).then_inc(s_tokA, 1)

            def square(b, c):
                act.wait_ge(s_cc, at(b, c))
                act.activation(half(slot(b, K0), c), half(ps[b][1], c), ACT.Square).then_inc(s_sq, 1)

            def rstd(b, c):
                act.wait_ge(s_var, at(b, c))
                act.activation(half(slot(b, K1), c), half(ps[b][0], c), ACT.Ln, bias=ceps[:, 0:1]).then_inc(s_ln, 1)
                act.wait_ge(s_ln, at(b, c))
                act.activation(half(slot(b, K1), c), half(slot(b, K1), c), ACT.Exp, scale=-0.5).then_inc(s_rstd, 1)

            def swish(b):
                act.preload_act_table_set("silu_and_others")
                for c in range(2):
                    act.wait_ge(s_xc, at(b, c))
                    act.activation(half(u[b], c), half(ps[b][1], c), ACT.Silu, bias=cb[:, 0:1]).then_inc(s_u, 1)
                for c in range(2):
                    act.wait_ge(s_res, b + 1)
                    act.activation(half(gate[b], c), half(ps[b][0], c), ACT.Silu).then_inc(s_gate, 1)
                act.preload_act_table_set("natural_log_exp_and_others")

            def softplus(b, c):
                t = half(slot(b, K1), c)
                act.wait_ge(s_dz, back(b, c))
                step(act.activation(t, half(ps[b][1], c), ACT.Abs, bias=bdt[:, 0:1]))
                step(act.activation(t, t, ACT.Exp, scale=-1.0))
                act.activation(t, t, ACT.Ln, bias=1.0).then_inc(s_spl, 1)

            def decay(b):
                for c in range(2):
                    act.wait_ge(s_R, back(b, c))
                    act.activation(half(slot(b, K1), c, LR), half(slot(b, K3), c, LR), ACT.Exp, scale=A[:, 0:1]
                                   ).then_inc(s_E, 1)

            def rdecay(b):
                for c in range(2):
                    act.wait_ge(s_E, at(b, c))
                    act.activation(half(rden[b], c, LR), half(slot(b, K1), c, LR), ACT.Ln, bias=ceps[:, 1:2]
                                   ).then_inc(s_lE, 1)
                for c in range(2):
                    act.wait_ge(s_lE, at(b, c))
                    act.activation(half(rden[b], c, LR), half(rden[b], c, LR), ACT.Exp, scale=-1.0).then_inc(s_rE, 1)

            def tail_decay(b):
                e, r = xn[b][:, 0:NS * TL], rtail[b]
                act.wait_ge(s_argT, b + 1)
                act.activation(e, e, ACT.Exp).then_inc(s_ET, 1)
                act.wait_ge(s_ET, b + 1)
                step(act.activation(r, e, ACT.Ln, bias=ceps[:, 1:2]))
                act.activation(r, r, ACT.Exp, scale=-1.0).then_inc(s_rET, 1)

            def general(b):
                act.wait_ge(s_flag, b + 1)
                lanes = act.value_load(count[0:1, b:b + 1], min_val=0, max_val=128)
                with act.If(lanes < 128):
                    act.wait_ge(s_y0, 2 * b + 2)
                    with act.Fori(1, NS) as n:
                        act.wait_ge(g_y[b], n)
                        act.activation(wcur[:, 0:1], wx[:, bass.ds(n + RK, 1)], ACT.Copy).then_inc(g_cp[b], 1)
                        act.activation(wcur[:, 1:2], wx[:, bass.ds(n + RK + NS, 1)], ACT.Copy).then_inc(g_cp[b], 1)
                        act.activation(acur[:, 0:1], A[:, bass.ds(n, 1)], ACT.Copy).then_inc(g_cp[b], 1)
                        act.wait_ge(g_cp[b], n * 3)
                        act.activation(slot(b, K1)[:, 0:LR], slot(b, K3)[:, 0:LR], ACT.Exp, scale=acur[:, 0:1]
                                       ).then_inc(g_E[b], 1)
                        act.wait_ge(g_E[b], n)
                        act.activation(rden[b][:, :], slot(b, K1)[:, 0:LR], ACT.Ln, bias=ceps[:, 1:2]
                                       ).then_inc(g_L[b], 1)
                        act.wait_ge(g_L[b], n)
                        act.activation(rden[b][:, :], rden[b][:, :], ACT.Exp, scale=-1.0).then_inc(g_r[b], 1)

            def norm2(b, c):
                act.wait_ge(s_z2, at(b, c))
                act.activation(half(slot(b, K0), c)[64:128, :], half(ps[b][1], c)[64:128, :], ACT.Square).then_inc(s_sq2, 1)
                act.wait_ge(ld["s_ffnw"], 32)
                act.activation(half(h2[b], c)[0:DM, :], half(ps[b][1], c)[0:DM, :], ACT.Identity, bias=bob[:, 0:1]).then_inc(s_h2, 1)

            def rstd2(b, c):
                t = half(slot(b, K1), c)[64:128, :]
                act.wait_ge(s_var2, at(b, c))
                act.activation(t, half(ps[b][0], c)[64:128, :], ACT.Ln, bias=ceps[64:128, 0:1]).then_inc(s_ln2, 1)
                act.wait_ge(s_ln2, at(b, c))
                act.activation(t, t, ACT.Exp, scale=-0.5).then_inc(s_rstd2, 1)

            def relu_in(b, c):
                act.wait_ge(s_wi, at(b, c))
                act.activation(half(slot(b, K0), c), half(ps[b][1], c), ACT.Relu, bias=bib[:, 0:1]).then_inc(s_h1, 1)

            def relu(b, c, l):
                act.wait_ge(s_l1 if l == 0 else s_l2, at(b, c))
                act.activation(half(slot(b, K1), c), half(ps[b][0], c), ACT.Relu).then_inc(s_r1 if l == 0 else s_r2, 1)

            def ffn_copy(b, c, l):
                act.wait_ge(s_t1 if l == 0 else s_t2, at(b, c))
                act.activation(half(slot(b, K2 if l == 0 else K3), c), half(ps[b][1], c), ACT.Copy
                               ).then_inc(s_t1c if l == 0 else s_t2c, 1)

            def residual_rows(b, c):
                act.wait_ge(s_resid, at(b, c))
                act.activation(half(slot(b, K0), c)[:, 0:4 * DM], half(ps[b][1], c)[:, 0:4 * DM], ACT.Copy
                               ).then_inc(s_residc, 1)

            act.preload_act_table_set("natural_log_exp_and_others")
            weights()
            tokens(0, 0)
            tokens(0, 1)
            act.wait_ge(s_set, 1)
            square(0, 0)
            square(0, 1)
            rstd(0, 0)
            rstd(0, 1)
            decay_rates()
            tokens(1, 0)
            act.wait_ge(ld["s_convw"], 80)
            swish(0)
            softplus(0, 1)
            softplus(0, 0)
            tokens(1, 1)
            decay(0)
            rdecay(0)
            square(1, 0)
            square(1, 1)
            rstd(1, 0)
            rstd(1, 1)
            tail_decay(0)
            general(0)
            swish(1)
            softplus(1, 1)
            norm2(0, 0)
            softplus(1, 0)
            norm2(0, 1)
            rstd2(0, 0)
            rstd2(0, 1)
            decay(1)
            rdecay(1)
            relu_in(0, 0)
            general(1)
            relu_in(0, 1)
            tail_decay(1)
            relu(0, 0, 0)
            relu(0, 1, 0)
            ffn_copy(0, 0, 0)
            ffn_copy(0, 1, 0)
            relu(0, 0, 1)
            relu(0, 1, 1)
            norm2(1, 0)
            norm2(1, 1)
            rstd2(1, 0)
            rstd2(1, 1)
            residual_rows(0, 0)
            residual_rows(0, 1)
            relu_in(1, 0)
            relu_in(1, 1)
            relu(1, 0, 0)
            relu(1, 1, 0)
            relu(1, 0, 1)
            relu(1, 1, 1)
            residual_rows(1, 0)
            residual_rows(1, 1)

        @block.tensor
        def _(pe):
            mm = nc.tensor.matmul

            def halves(pair, lhsT, rhs, n=L, start=True, stop=True):
                for c in range(0, n, 512):
                    last = mm(pair[:, c:min(c + 512, n)], lhsT, rhs[:, c:min(c + 512, n)], start=start, stop=stop)
                return last

            def token_weights():
                pe.wait_ge(ld["s_tokw"], 64)
                pe.wait_ge(ld["s_const"], 16)
                for j in range(DM // 8):
                    last = mm(ps[0][0][:, 64 * j:64 * j + 64], wt[:, 128 * j:128 * j + 128],
                              cst[0:4 * RIF, C_DFT:C_DFT + 4 * PATCH], start=True, stop=True)
                last.then_inc(s_weff_mm, 1)

            def tokens(b, k):
                if b == 0:
                    pe.wait_ge(s_weff, 4)
                pe.wait_ge(ld[f"s_x{b}{k}"], 32 + 32 * k)
                for q in range(4):
                    last = mm(half(ps[b][0], k), weff[:, q, :, :], xs[:, b, 8 * k:8 * k + 8, V * q:V * q + V],
                              start=q == 0, stop=q == 3)
                last.then_inc(s_tok, 1)

            def tokens_last(b):
                if b == 1:
                    pe.wait_ge(s_exc, 8)
                pe.wait_ge(s_wlast, 1)
                mm(ps[b][1][:, 0:V], wlast[:, :], xlast[:, b, :], start=True, stop=True).then_inc(s_tok, 1)

            def small_weights():
                pe.wait_ge(ld["s_attw"], 96)
                nc.tensor.transpose(ps[1][1][0:RK, 0:DI], wx[:, 0:RK], ident)
                pe.wait_ge(ld["s_wio"], 48)
                nc.tensor.transpose(ps[1][1][:, 128:128 + HID], wi2[:, :, :], ident)
                nc.tensor.transpose(ps[1][1][:, 256:256 + DM], won[:, :], cst[0:DM, C_ID:C_ID + DM])
                pe.wait_ge(ld["s_ws"], 16)
                for l in range(NL):
                    last = nc.tensor.transpose(ps[1][1][:, 512 + HID * l:512 + HID * l + HID], wsh[:, l, :], ident)
                last.then_inc(s_wtr, 1)

            def delta_weights():
                pe.wait_ge(s_wtrc, 1)
                mm(ps[1][1][:, 384:384 + DI], wxT[:, :], wdt[:, :], start=True, stop=True).then_inc(s_wd, 1)

            def centered(b, c):
                pe.wait_ge(s_tokA, 2 * b + 2)
                pe.wait_ge(s_tokB, 3 * b + 3)
                for late in range(2):
                    last = mm(half(ps[b][1], c)[64 * late:64 * late + 64, :], c_cc,
                              tok[b][:, HL * c + 1 - late:HL * c + HL + 1 - late], start=True, stop=True)
                last.then_inc(s_cc, 1)

            def variance(b, c):
                pe.wait_ge(s_sq, at(b, c))
                mm(half(ps[b][0], c), c_bd, half(slot(b, K0), c), start=True, stop=True).then_inc(s_var, 1)

            def conv(b, c):
                pe.wait_ge(s_wconv, 1)
                pe.wait_ge(s_xn, at(b, c))
                to = HL * c
                mm(half(ps[b][1], c), w_conv[:, 1, :], xn[b][:, to + 2:to + 2 + HL], start=True, stop=False)
                mm(half(ps[b][1], c), w_conv[:, 0, :], xn[b][:, to:to + HL], start=False, stop=True).then_inc(s_xc, 1)

            def residual(b):
                pe.wait_ge(s_xn, 2 * b + 2)
                for c in range(2):
                    rows, first = slice(64 * (1 - c), 64 * (1 - c) + 64), HL * c + 3 - c
                    last = mm(half(ps[b][0], c), w_in2[rows, DI:2 * DI], xn[b][rows, first:first + HL],
                              start=True, stop=True)
                last.then_inc(s_res, 1)

            def delta(b, c):
                pe.wait_ge(s_prep, 1)
                pe.wait_ge(s_u, 2 * b + 2)
                mm(half(ps[b][1], c), wdelta[:, :], half(u[b], c), start=True, stop=True).then_inc(s_dz, 1)

            def first_state(b):
                for c in range(2):
                    pe.wait_ge(s_gate, at(b, c))
                    mm(half(ps[b][0], c, LR), bc(wx[:, RK:RK + 1], [DI, 128]), half(u[b], c, LR),
                       start=True, stop=True).then_inc(s_B0, 1)

            def first_state_c(b):
                pe.wait_ge(s_dl, 2 * b + 2)
                pe.wait_ge(s_flag, b + 1)
                for c in range(2):
                    mm(half(ps[b][1], c, LR), bc(wx[:, RK + NS:RK + NS + 1], [DI, 128]), half(u[b], c, LR),
                       start=True, stop=True).then_inc(s_C0, 1)

            def safe_lanes(b):
                pe.wait_ge(s_safe, b + 1)
                mm(ps[b][1][0:1, LR + 4:LR + 5], safe[:, b:b + 1], onecol[:, :], start=True, stop=True).then_inc(s_cnt, 1)

            def tail(b):
                pe.wait_ge(s_w, 2 * b + 2)
                pe.wait_ge(s_tprod, b + 1)
                for c in range(2):
                    last = mm(half(ps[b][0], c), ones, half(tprod[b], c), start=True, stop=True)
                last.then_inc(s_tl, 1)

            def general(b):
                pe.wait_ge(s_flag, b + 1)
                lanes = pe.value_load(count[0:1, b:b + 1], min_val=0, max_val=128)
                with pe.If(lanes < 128):
                    pe.wait_ge(s_y0, 2 * b + 2)
                    with pe.Fori(1, NS) as n:
                        pe.wait_ge(g_cp[b], n * 3)
                        pe.wait_ge(g_y[b], n)
                        halves(ps[b][1], bc(wcur[:, 0:1], [DI, 128]), u[b], LR).then_inc(g_B[b], 1)
                        pe.wait_ge(g_w[b], n)
                        halves(ps[b][1], bc(wcur[:, 1:2], [DI, 128]), u[b], LR).then_inc(g_C[b], 1)

            def attention_out(b, c):
                pe.wait_ge(s_ysum, 2 * b + 1)
                mm(half(ps[b][1], c), c_ic, tok[b][:, HL * c + 1:HL * c + 1 + HL], start=True, stop=False)
                pe.wait_ge(s_yg, at(b, c))
                mm(half(ps[b][1], c), wout[:, :, :], half(slot(b, K1), c), start=False, stop=True).then_inc(s_z2, 1)

            def variance2(b, c):
                pe.wait_ge(s_sq2, at(b, c))
                mm(half(ps[b][0], c)[64:128, :], c_bd[64:128, 64:128], half(slot(b, K0), c)[64:128, :],
                   start=True, stop=True).then_inc(s_var2, 1)

            def ffn_in(b, c):
                pe.wait_ge(s_h2, at(b, c))
                pe.wait_ge(s_xn2, at(b, c))
                mm(half(ps[b][1], c), wiT[64:128, :], half(slot(b, K2), c)[64:128, :], start=True, stop=True
                   ).then_inc(s_wi, 1)

            def ffn_layer(b, c, l):
                if l == 0:
                    h = half(slot(b, K0), c)
                    pe.wait_ge(s_bparts, 1)
                    pe.wait_ge(s_onehot, 1)
                    pe.wait_ge(s_h1, at(b, c))
                    if c == 0:
                        pe.wait_ge(s_sel0, GB // 2 * (b + 1))
                    else:
                        pe.wait_ge(s_sel1[b], 16 * GB // 2)
                else:
                    h = half(slot(b, K2), c)
                    pe.wait_ge(s_t1c, at(b, c))
                per, g0 = 128 // GT, (2 * b + c) * GB // 2
                to = half(ps[b][0], c)
                for i in range(4):
                    mm(to[:, 128 * i:128 * i + 128], onehott[:, g0 + per * i:g0 + per * i + per, :], bparts[:, l, :],
                       start=i == 0, stop=False, skip_group_check=True)
                for i in range(4):
                    for k in range(per):
                        t = 128 * i + GT * k
                        last = mm(to[GT * k:GT * k + GT, 128 * i:128 * i + 128], h[:, t:t + GT],
                                  wsel[:, g0 + per * i + k, l, :], start=False, stop=True, skip_group_check=True)
                last.then_inc(s_l1 if l == 0 else s_l2, 1)

            def ffn_turn(b, c, l):
                pe.wait_ge(s_r1 if l == 0 else s_r2, at(b, c))
                for i in range(4):
                    cols = slice(HL * c + 128 * i, HL * c + 128 * i + 128)
                    last = nc.tensor.transpose(ps[b][1][:, cols], slot(b, K1)[:, cols], ident)
                last.then_inc(s_t1 if l == 0 else s_t2, 1)

            def ffn_out(b, c):
                hv = half(slot(b, K3), c).rearrange("p (t j) -> p j t", j=4)
                rv = half(h2[b], c).rearrange("p (t j) -> p j t", j=4)
                to = half(ps[b][0], c)
                pe.wait_ge(s_t2c, at(b, c))
                for j in range(4):
                    last = nc.tensor.transpose(half(ps[b][1], c)[:, DM * j:DM * j + DM], rv[:, j, :], cst[0:DM, C_ID:C_ID + DM])
                last.then_inc(s_resid, 1)
                for j in range(4):
                    last = mm(to[:, DM * j:DM * j + DM], hv[:, j, :], woT[:, :], start=True, stop=True)
                last.then_inc(s_fin, 1)

            def experts(k):
                l, e = k // 4, 4 * (k % 4)
                pe.wait_ge(ld[f"s_wr{k // 2}"], 16)
                pe.wait_ge(s_prep, 1)
                if k >= 2:
                    pe.wait_ge(s_exc, k - 1)
                for i in range(4):
                    last = nc.tensor.transpose(half(ps[1][1], k % 2)[:, 128 * i:128 * i + 128], wrn[:, l, e + i, :], ident)
                last.then_inc(s_ex, 1)

            def keep_warm(n, bank):
                for _ in range(n):
                    mm(bank, warm[:, 0:128], warm[:, :], start=True, stop=True)

            pe.wait_ge(s_warm, 1)
            keep_warm(12, ps[1][0][:, 0:HL])
            token_weights()
            keep_warm(5, ps[1][0][:, 0:HL])
            tokens(0, 0)
            tokens(0, 1)
            tokens_last(0)
            centered(0, 0)
            centered(0, 1)
            variance(0, 0)
            variance(0, 1)
            small_weights()
            tokens(1, 0)
            delta_weights()
            conv(0, 0)
            experts(0)
            experts(1)
            conv(0, 1)
            experts(2)
            experts(3)
            residual(0)
            experts(4)
            delta(0, 1)
            experts(5)
            experts(6)
            delta(0, 0)
            experts(7)
            tokens(1, 1)
            tokens_last(1)
            first_state(0)
            safe_lanes(0)
            first_state_c(0)
            centered(1, 0)
            centered(1, 1)
            variance(1, 0)
            variance(1, 1)
            tail(0)
            general(0)
            conv(1, 0)
            conv(1, 1)
            residual(1)
            delta(1, 1)
            delta(1, 0)
            attention_out(0, 0)
            attention_out(0, 1)
            first_state(1)
            variance2(0, 0)
            safe_lanes(1)
            variance2(0, 1)
            first_state_c(1)
            ffn_in(0, 0)
            ffn_in(0, 1)
            tail(1)
            general(1)
            ffn_layer(0, 0, 0)
            ffn_layer(0, 1, 0)
            ffn_turn(0, 0, 0)
            ffn_turn(0, 1, 0)
            attention_out(1, 0)
            ffn_layer(0, 0, 1)
            ffn_layer(0, 1, 1)
            ffn_turn(0, 0, 1)
            attention_out(1, 1)
            ffn_turn(0, 1, 1)
            variance2(1, 0)
            variance2(1, 1)
            ffn_out(0, 0)
            ffn_out(0, 1)
            ffn_in(1, 0)
            ffn_in(1, 1)
            ffn_layer(1, 0, 0)
            ffn_layer(1, 1, 0)
            ffn_turn(1, 0, 0)
            ffn_turn(1, 1, 0)
            ffn_layer(1, 0, 1)
            ffn_layer(1, 1, 1)
            ffn_turn(1, 0, 1)
            ffn_turn(1, 1, 1)
            ffn_out(1, 0)
            ffn_out(1, 1)

        @block.vector
        def _(dve):
            v = nc.vector
            steps = [0]

            def step(ins):
                ins.then_inc(s_v, 1)
                steps[0] += 1
                dve.wait_ge(s_v, steps[0])

            def constants():
                v.memset(warm[:, :], 0.0).then_inc(s_warm, 1)
                v.memset(onecol[:, :], 1.0)
                v.memset(ceps[:, 0:1], LN_EPS)
                for b in range(B):
                    v.memset(xn[b][:, 0:2], 0.0)
                    v.memset(tok[b][:, 0:1], 0.0)
                v.memset(brest[:, :, :], 0.0)
                v.memset(ceps[:, 1:2], E_EPS).then_inc(s_set, 1)

            def token_weights():
                dve.wait_ge(s_weff_mm, 1)
                for h in range(2):
                    v.tensor_copy(weff_to(h, 1), weff_from(h, 1)).then_inc(s_weff, 1)
                dve.wait_ge(s_weff, 4)
                v.reduce_sum(wlast[:, :], weff[:, :, :, :].rearrange("p q a o -> p (a o) q"), AX.X).then_inc(s_wlast, 1)

            def conv_weights():
                dve.wait_ge(ld["s_convw"], 80)
                v.tensor_tensor(w_conv[:, :, :], bc(w_in2[:, 0:DI].unsqueeze(1), [128, 2, DI]), taps[:, :, :], ALU.mult
                                ).then_inc(s_wconv, 1)

            def small_weights():
                dve.wait_ge(s_wtr, 1)
                v.tensor_copy(wxT[:, :], ps[1][1][0:RK, 0:DI])
                v.tensor_copy(wiT[:, :], ps[1][1][:, 128:128 + HID])
                v.tensor_copy(woT[:, :], ps[1][1][:, 256:256 + DM]).then_inc(s_wtrc, 1)
                v.tensor_tensor(wsh[:, :, :], ps[1][1][:, 512:512 + NL * HID].rearrange("p (l h) -> p l h", h=HID),
                                bc(ident.unsqueeze(1), [HID, NL, HID]), ALU.add)
                v.tensor_scalar(nbdt[:, :], bdt[:, :], -1.0, None, ALU.mult)
                step(v.reduce_sum(wmean[:, :], wout[:, 0, :], AX.X))
                step(v.tensor_scalar(wmean[:, :], wmean[:, :], 1.0 / DM, None, ALU.mult))
                v.tensor_scalar(wout[:, 1, :], wout[:, 0, :], wmean[:, 0:1], None, ALU.subtract)

            def routes():
                dve.wait_ge(s_A, 1)
                v.reduce_max(amax[:, :], A[:, 1:NS], AX.X)
                dve.wait_ge(ld["s_route"], 32)
                step(v.tensor_scalar(onehot[:, :], ridb[:, :], cst[0:96, C_IOTA:C_IOTA + 1],
                                     cst[0:96, C_SHARED:C_SHARED + 1], ALU.is_equal, ALU.add))
                v.tensor_copy(onehott[:, :, :], bc(onehot[:, :].unsqueeze(2), [96, NG, GT])).then_inc(s_onehot, 1)

            def delta_weights():
                dve.wait_ge(s_wd, 1)
                v.tensor_copy(wdelta[:, :], ps[1][1][:, 384:384 + DI]).then_inc(s_prep, 1)

            def tokens(b, k):
                to = tok[b][64:128, 1:].rearrange("p (v n) -> p n v", n=NP)
                first, src = ((0, ps[b][0][64:128, V:HL]), (7, ps[b][0][64:128, HL:L]), (15, ps[b][1][64:128, 0:V]))[k]
                src = src.rearrange("p (n v) -> p n v", v=V)
                dve.wait_ge(s_tok, 3 * b + k + 1)
                v.tensor_copy(to[:, first:first + src.shape[1], :], src).then_inc(s_tokB, 1)

            def experts(k):
                l, e = k // 4, 4 * (k % 4)
                dve.wait_ge(s_ex, k + 1)
                v.tensor_tensor(wexp[:, e:e + 4, l, :], half(ps[1][1], k % 2).rearrange("p (e h) -> p e h", h=HID),
                                bc(wsh[:, l:l + 1, :], [HID, 4, HID]), ALU.add).then_inc(s_exc, 1)

            def norm(b, c):
                dve.wait_ge(s_rstd, at(b, c))
                v.tensor_tensor(xn[b][:, HL * c + 2:HL * c + HL + 2], half(ps[b][1], c), half(slot(b, K1), c), ALU.mult
                                ).then_inc(s_xn, 1)

            def steps_sum(b):
                R, d = slot(b, K3), slot(b, K0)
                v.memset(R[:, L - 1:L], 0.0)
                for c in (1, 0):
                    dve.wait_ge(s_spl, back(b, c))
                    v.scalar_tensor_tensor(half(d, c), half(ps[b][1], c), nbdt[:, 0:1], half(slot(b, K1), c),
                                           ALU.max, ALU.add).then_inc(s_dl, 1)
                    dve.wait_ge(s_dl, back(b, c))
                    if c == 1:
                        v.tensor_tensor_scan(R[:, HL:L - 1][:, ::-1], d[:, HL + 1:L][:, ::-1],
                                             bc(bdt[:, 0:1], [128, HL - 1]), 0.0, ALU.add, ALU.add).then_inc(s_R, 1)
                    else:
                        v.tensor_tensor_scan(R[:, 0:HL][:, ::-1], d[:, 1:HL + 1][:, ::-1],
                                             bc(bdt[:, 0:1], [128, HL]), R[:, HL:HL + 1], ALU.add, ALU.add
                                             ).then_inc(s_R, 1)
                        v.tensor_scalar(safe[:, b:b + 1], R[:, LR - 1:LR], amax[:, 0:1], ZERO_EXP, ALU.mult, ALU.is_le
                                        ).then_inc(s_safe, 1)
                    v.scalar_tensor_tensor(half(slot(b, K2), c), half(d, c), bdt[:, 0:1], half(u[b], c), ALU.add, ALU.mult
                                           ).then_inc(s_du, 1)
                    dve.wait_ge(s_R, back(b, c))

            def counted(b):
                dve.wait_ge(s_cnt, b + 1)
                v.tensor_copy(count[0:1, b:b + 1], ps[b][1][0:1, LR + 4:LR + 5]).then_inc(s_flag, 1)

            def first_sums(b):
                w = slot(b, K0)
                dve.wait_ge(s_du, 2 * b + 2)
                for c in range(2):
                    dve.wait_ge(s_B0, at(b, c))
                    v.tensor_tensor(half(w, c, LR), half(ps[b][0], c, LR), half(slot(b, K2), c, LR), ALU.mult).then_inc(s_w, 1)
                dve.wait_ge(s_flag, b + 1)
                lanes = dve.value_load(count[0:1, b:b + 1], min_val=0, max_val=128)
                for c in range(2):
                    dve.wait_ge(s_w, at(b, c))
                    dve.wait_ge(s_E, at(b, c))
                    v.tensor_tensor(half(w, c, LR), half(w, c, LR), half(slot(b, K1), c, LR), ALU.mult).then_inc(s_wE, 1)
                for c in range(2):
                    wc = half(w, c, LR)
                    dve.wait_ge(s_wE, at(b, c))
                    if c == 1:
                        dve.wait_ge(s_sum, 2 * b + 1)
                    v.tensor_tensor_scan(wc, bc(onecol[:, 0:1], [128, wc.shape[1]]), wc,
                                         0.0 if c == 0 else w[:, HL - 1:HL], ALU.mult, ALU.add).then_inc(s_sum, 1)
                dve.wait_ge(s_sum, 2 * b + 2)
                dve.wait_ge(s_setx, 2)
                v.tensor_copy(carry[:, b, 0:1], w[:, LR - 1:LR]).then_inc(s_carry, 1)
                return lanes

            def first_state(b):
                w = slot(b, K0)
                dve.wait_ge(s_carry, b + 1)
                for c in range(2):
                    dve.wait_ge(s_rE, at(b, c))
                    v.tensor_tensor(half(w, c, LR), half(w, c, LR), half(rden[b], c, LR), ALU.mult).then_inc(s_wr, 1)
                for c in range(2):
                    dve.wait_ge(s_wr, at(b, c))
                    dve.wait_ge(s_C0, at(b, c))
                    v.tensor_tensor(half(w, c, LR), half(w, c, LR), half(ps[b][1], c, LR), ALU.mult).then_inc(s_y0, 1)
                dve.wait_ge(s_y0, 2 * b + 2)

            def general(b, lanes):
                y, E = slot(b, K0)[:, 0:LR], slot(b, K1)[:, 0:LR]
                with dve.If(lanes < 128):
                    v.memset(gbuf[:, 0:1], 0.0).then_inc(g_y[b], 1)
                    dve.wait_ge(g_y[b], 1)
                    with dve.Fori(1, NS) as n:
                        dve.wait_ge(g_B[b], n)
                        v.tensor_tensor(gbuf, ps[b][1][:, 0:LR], slot(b, K2)[:, 0:LR], ALU.mult
                                        ).then_inc(g_w[b], 1)
                        dve.wait_ge(g_w[b], n)
                        dve.wait_ge(g_E[b], n)
                        v.tensor_tensor(gbuf, gbuf, E, ALU.mult).then_inc(g_v[b], 1)
                        dve.wait_ge(g_v[b], n * 4 - 3)
                        v.tensor_tensor_scan(gbuf, bc(onecol[:, 0:1], [128, LR]), gbuf, 0.0,
                                             ALU.mult, ALU.add).then_inc(g_v[b], 1)
                        dve.wait_ge(g_v[b], n * 4 - 2)
                        v.tensor_copy(carry[:, b, bass.ds(n, 1)], gbuf[:, LR - 1:LR]).then_inc(g_v[b], 1)
                        dve.wait_ge(g_v[b], n * 4 - 1)
                        dve.wait_ge(g_r[b], n)
                        v.tensor_tensor(gbuf, gbuf, rden[b][:, :], ALU.mult).then_inc(g_v[b], 1)
                        dve.wait_ge(g_v[b], n * 4)
                        dve.wait_ge(g_C[b], n)
                        v.tensor_tensor(gbuf, gbuf, ps[b][1][:, 0:LR], ALU.mult).then_inc(g_m[b], 1)
                        dve.wait_ge(g_m[b], n)
                        v.tensor_tensor(y, y, gbuf, ALU.add).then_inc(g_y[b], 1)
                        dve.wait_ge(g_y[b], n + 1)

            def tail_gated(b):
                E = xn[b][:, 0:NS * TL]
                w = xn[b][:, NS * TL:2 * NS * TL]
                w3 = w.rearrange("p (n t) -> p n t", t=TL)
                bt = ps[b][0][:, :].rearrange("p (t c n) -> p c n t", c=2, n=NS)
                y, yg, ub, gb = slot(b, K0), slot(b, K1), u[b], gate[b]
                before = 6 * b

                def past(steps):
                    dve.wait_ge(s_tail, before + steps)
                v.scalar_tensor_tensor(y[:, 0:HL], ub[:, 0:HL], dpar[:, 0:1], y[:, 0:HL], ALU.mult, ALU.add).then_inc(s_ysum, 1)
                dve.wait_ge(s_tl, b + 1)
                v.tensor_tensor(w3, bt[:, 0], bc(slot(b, K2)[:, LR:L].unsqueeze(1), [128, NS, TL]), ALU.mult).then_inc(s_tail, 1)
                dve.wait_ge(s_ysum, 2 * b + 1)
                v.tensor_tensor(yg[:, 0:HL], y[:, 0:HL], gb[:, 0:HL], ALU.mult).then_inc(s_yg, 1)
                past(1)
                dve.wait_ge(s_ET, b + 1)
                v.tensor_tensor(w, w, E, ALU.mult).then_inc(s_tail, 1)
                v.scalar_tensor_tensor(y[:, HL:LR], ub[:, HL:LR], dpar[:, 0:1], y[:, HL:LR], ALU.mult, ALU.add).then_inc(s_ysum, 1)
                past(2)
                v.tensor_tensor(w3[:, :, 0], w3[:, :, 0], carry[:, b, :], ALU.add).then_inc(s_tail, 1)
                dve.wait_ge(s_ysum, 2 * b + 2)
                v.tensor_tensor(yg[:, HL:LR], y[:, HL:LR], gb[:, HL:LR], ALU.mult)
                past(3)
                v.tensor_tensor_scan(w, seg[:, :, :].rearrange("p n t -> p (n t)"), w, 0.0, ALU.mult, ALU.add).then_inc(s_tail, 1)
                past(4)
                dve.wait_ge(s_rET, b + 1)
                v.tensor_tensor(w, w, rtail[b], ALU.mult).then_inc(s_tail, 1)
                past(5)
                v.tensor_tensor(w3, w3, bt[:, 1], ALU.mult).then_inc(s_tail, 1)
                past(6)
                step(v.reduce_sum(ytail[:, b, :], w3.rearrange("p n t -> p t n"), AX.X))
                step(v.scalar_tensor_tensor(y[:, LR:L], ub[:, LR:L], dpar[:, 0:1], ytail[:, b, :], ALU.mult, ALU.add))
                v.tensor_tensor(yg[:, LR:L], y[:, LR:L], gb[:, LR:L], ALU.mult).then_inc(s_yg, 1)

            def ffn_copy(b, c, l):
                dve.wait_ge(s_t1 if l == 0 else s_t2, at(b, c))
                v.tensor_copy(half(slot(b, K2 if l == 0 else K3), c), half(ps[b][1], c)
                              ).then_inc(s_t1c if l == 0 else s_t2c, 1)

            def norm2(b, c):
                dve.wait_ge(s_rstd2, at(b, c))
                v.tensor_tensor(half(slot(b, K2), c)[64:128, :], half(ps[b][1], c)[64:128, :],
                                half(slot(b, K1), c)[64:128, :], ALU.mult).then_inc(s_xn2, 1)

            def out_add(b, c):
                dve.wait_ge(s_fin, at(b, c))
                dve.wait_ge(s_residc, at(b, c))
                rows = half(slot(b, K0), c)[:, 0:4 * DM]
                v.tensor_tensor(rows, rows, half(ps[b][0], c)[:, 0:4 * DM], ALU.add).then_inc(s_oc, 1)

            constants()
            token_weights()
            tokens(0, 0)
            conv_weights()
            tokens(0, 1)
            tokens(0, 2)
            small_weights()
            norm(0, 0)
            norm(0, 1)
            delta_weights()
            tokens(1, 0)
            routes()
            experts(0)
            experts(1)
            experts(2)
            experts(3)
            experts(4)
            experts(5)
            experts(6)
            experts(7)
            steps_sum(0)
            counted(0)
            tokens(1, 1)
            tokens(1, 2)
            lanes = first_sums(0)
            norm(1, 0)
            norm(1, 1)
            first_state(0)
            general(0, lanes)
            tail_gated(0)
            steps_sum(1)
            counted(1)
            norm2(0, 0)
            norm2(0, 1)
            lanes = first_sums(1)
            first_state(1)
            general(1, lanes)
            tail_gated(1)
            ffn_copy(0, 0, 1)
            ffn_copy(0, 1, 1)
            norm2(1, 0)
            norm2(1, 1)
            out_add(0, 0)
            out_add(0, 1)
            ffn_copy(1, 0, 0)
            ffn_copy(1, 1, 0)
            ffn_copy(1, 0, 1)
            ffn_copy(1, 1, 1)
            out_add(1, 0)
            out_add(1, 1)


_INS = ["x", "L0_tok_W", "L0_attn_W_in", "L0_attn_conv_k", "L0_attn_conv_b", "L0_attn_W_x", "L0_attn_W_dt",
        "L0_attn_b_dt", "L0_attn_A_log", "L0_attn_D_param", "L0_attn_W_out", "L0_ffn_route_id", "L0_ffn_Wi",
        "L0_ffn_bi", "L0_ffn_Wr", "L0_ffn_br", "L0_ffn_Ws", "L0_ffn_bs", "L0_ffn_Wo", "L0_ffn_bo"]


def shape_constants():
    import numpy as np

    c = np.zeros((128, C_ALL), np.float32)
    eye, mean = np.eye(DM), np.full((DM, DM), 1.0 / DM)
    c[:, C_ID:C_ID + 128] = np.eye(128)
    c[:, C_CC:C_CC + DM] = np.tile(eye - mean, (2, 1))
    c[:, C_BD:C_BD + 128] = np.kron(np.eye(2), mean)
    c[:, C_IC:C_IC + 128] = np.tile(np.hstack([eye, eye - mean]), (2, 1))
    angle = 2 * np.pi * np.outer(np.arange(NF), np.arange(PATCH)) / PATCH
    dft = np.vstack([np.cos(angle), -np.sin(angle)]) / np.sqrt(PATCH)
    dft = dft.reshape(RIF, 2, 2, 4).transpose(0, 2, 3, 1).reshape(RIF, PATCH)
    for k in range(4):
        c[RIF * k:RIF * k + RIF, C_DFT + PATCH * k:C_DFT + PATCH * k + PATCH] = dft
    row = np.arange(128) % 32
    c[:, C_IOTA] = np.where(row < NE, row, -1)
    c[:, C_SHARED] = row == NE
    return c


def kernel(**inputs):
    import numpy as np
    import concourse.bacc as bacc
    from concourse.bass_utils import run_bass_kernel_spmd

    nc = bacc.Bacc("TRN2", target_bir_lowering=False, num_devices=1)
    arrays, args = {}, []
    for name in _INS:
        a = np.ascontiguousarray(inputs[name])
        arrays[f"in_{name}"] = a
        args.append(nc.dram_tensor(f"in_{name}", a.shape, mybir.dt.from_np(a.dtype), kind="ExternalInput").ap())
    c = shape_constants()
    arrays["shape_constants"] = c
    args.append(nc.dram_tensor("shape_constants", c.shape, mybir.dt.float32, kind="ExternalInput").ap())
    args.append(nc.dram_tensor("out_tokens", (B, L, DM), mybir.dt.float32, kind="ExternalOutput").ap())
    tower(nc, *args)
    r = run_bass_kernel_spmd(nc, [arrays], core_ids=[0])
    return r.results[0]["out_tokens"]
```
